# Optimizing a Trainium2 kernel written in Bass

```python
import numpy as np
import jax
import jax.numpy as jnp

def _softmax(x, axis=-1):
    return jax.nn.softmax(x, axis=axis)

def _gelu(x):
    return jax.nn.gelu(x, approximate=True)

def _silu(x):
    return jax.nn.silu(x)

def _sigmoid(x):
    return jax.nn.sigmoid(x)

def _layernorm(x, axis=-1, eps=1e-05):
    m = jnp.mean(x, axis=axis, keepdims=True)
    v = jnp.var(x, axis=axis, keepdims=True)
    return (x - m) / jnp.sqrt(v + eps)

def _scatter_add(tgt, idx, src, axis=0):
    return tgt.at[idx].add(src)

def _segment_sum(src, seg, n):
    return jax.ops.segment_sum(src, seg, n)
kernel_name = 'mk_gnn_ffn_d1_gnn_r8_3adfca'

def setup_inputs(seed: int=0):
    np.random.seed(seed)
    _w = jnp.asarray

    def _rec_inputs():
        import jax
        import jax.numpy as jnp
        _gk = jax.random.key(seed)
        x = -0.0002117 + 1 * jax.random.normal(jax.random.fold_in(_gk, 1), (12500, 256), jnp.float32)
        src = jax.random.randint(jax.random.fold_in(_gk, 2), (200000,), 0, 12500, jnp.int32)
        dst = jnp.minimum((12500 * jax.random.uniform(jax.random.fold_in(_gk, 3), (200000,)) ** 2.0).astype(jnp.int32), 99999)
        _o = jnp.argsort(dst, stable=True)
        src = src[_o]
        dst = dst[_o]
        return (x, src, dst)
    x, src, dst = _rec_inputs()

    def _L0_gnn_setup():
        import jax, jax.numpy as jnp
        import numpy as np
        N = 12500
        E = 200000
        IN_FEATS = 256
        OUT_FEATS = 256
        MAXK = 32

        def _maxk(x, k):
            _, idx = jax.lax.top_k(x, k)
            rows = jnp.arange(x.shape[0])[:, None]
            mask = jnp.zeros_like(x).at[rows, idx].set(1.0)
            return x * mask
        key = jax.random.key(seed)
        k1, k2, k3, k4, k5 = jax.random.split(key, 5)
        feat = jax.random.normal(k1, (N, IN_FEATS), dtype=jnp.float32)
        W_self = jax.random.normal(k2, (IN_FEATS, OUT_FEATS), dtype=jnp.float32) * (1.0 / np.sqrt(IN_FEATS))
        W_neigh = jax.random.normal(k3, (IN_FEATS, OUT_FEATS), dtype=jnp.float32) * (1.0 / np.sqrt(IN_FEATS))
        src = jax.random.randint(k4, (E,), 0, N, dtype=jnp.int64)
        dst = jax.random.randint(k5, (E,), 0, N, dtype=jnp.int64)
        return {'feat': feat, 'W_self': W_self, 'W_neigh': W_neigh, 'src': src, 'dst': dst}
    _L0_gnn_all = _L0_gnn_setup()
    _L0_gnn_in = {k: v for k, v in _L0_gnn_all.items() if k in ('W_self', 'W_neigh')}
    del _L0_gnn_all

    def _L0_ffn_setup():
        import jax, jax.numpy as jnp
        import numpy as np
        DIM = 256
        H = 8
        D = 64
        G = 64
        INNER = H * D
        SCALE = D ** (-0.5)
        key = jax.random.key(seed)
        ks = jax.random.split(key, 12)
        B, N = (4, 2048)
        x = jax.random.normal(ks[0], (B, N, DIM), dtype=jnp.float32)
        s = lambda fan_in: 1.0 / np.sqrt(fan_in)
        W_fx = jax.random.normal(ks[1], (DIM, INNER), dtype=jnp.float32) * s(DIM)
        b_fx = jnp.zeros((INNER,), dtype=jnp.float32)
        W_x = jax.random.normal(ks[2], (DIM, INNER), dtype=jnp.float32) * s(DIM)
        b_x = jnp.zeros((INNER,), dtype=jnp.float32)
        A = jax.random.normal(ks[3], (G, D), dtype=jnp.float32)
        Q, _ = jnp.linalg.qr(A.T)
        W_slice = Q[:, :G].astype(jnp.float32)
        b_slice = jnp.zeros((G,), dtype=jnp.float32)
        W_q = jax.random.normal(ks[4], (D, D), dtype=jnp.float32) * s(D)
        W_k = jax.random.normal(ks[5], (D, D), dtype=jnp.float32) * s(D)
        W_v = jax.random.normal(ks[6], (D, D), dtype=jnp.float32) * s(D)
        W_out = jax.random.normal(ks[7], (INNER, DIM), dtype=jnp.float32) * s(INNER)
        b_out = jnp.zeros((DIM,), dtype=jnp.float32)
        temperature = jnp.ones((1, H, 1, 1), dtype=jnp.float32) * 0.5
        return {'x': x, 'W_fx': W_fx, 'b_fx': b_fx, 'W_x': W_x, 'b_x': b_x, 'W_slice': W_slice, 'b_slice': b_slice, 'W_q': W_q, 'W_k': W_k, 'W_v': W_v, 'W_out': W_out, 'b_out': b_out, 'temperature': temperature}
    _L0_ffn_all = _L0_ffn_setup()
    _L0_ffn_in = {k: v for k, v in _L0_ffn_all.items() if k in ('W_fx', 'b_fx', 'W_x', 'b_x', 'W_slice', 'b_slice', 'W_q', 'W_k', 'W_v', 'W_out', 'b_out', 'temperature')}
    del _L0_ffn_all
    return {'x': x, 'src': src, 'dst': dst, 'L0_gnn_W_self': _L0_gnn_in['W_self'], 'L0_gnn_W_neigh': _L0_gnn_in['W_neigh'], 'L0_ffn_W_fx': _L0_ffn_in['W_fx'], 'L0_ffn_b_fx': _L0_ffn_in['b_fx'], 'L0_ffn_W_x': _L0_ffn_in['W_x'], 'L0_ffn_b_x': _L0_ffn_in['b_x'], 'L0_ffn_W_slice': _L0_ffn_in['W_slice'], 'L0_ffn_b_slice': _L0_ffn_in['b_slice'], 'L0_ffn_W_q': _L0_ffn_in['W_q'], 'L0_ffn_W_k': _L0_ffn_in['W_k'], 'L0_ffn_W_v': _L0_ffn_in['W_v'], 'L0_ffn_W_out': _L0_ffn_in['W_out'], 'L0_ffn_b_out': _L0_ffn_in['b_out'], 'L0_ffn_temperature': _L0_ffn_in['temperature']}

def reference(x, src, dst, L0_gnn_W_self, L0_gnn_W_neigh, L0_ffn_W_fx, L0_ffn_b_fx, L0_ffn_W_x, L0_ffn_b_x, L0_ffn_W_slice, L0_ffn_b_slice, L0_ffn_W_q, L0_ffn_W_k, L0_ffn_W_v, L0_ffn_W_out, L0_ffn_b_out, L0_ffn_temperature):
    import jax
    import jax.numpy as jnp

    def _L0_gnn_ref(feat, W_self, W_neigh, src, dst):
        import jax, jax.numpy as jnp
        import numpy as np
        N = 12500
        E = 200000
        IN_FEATS = 256
        OUT_FEATS = 256
        MAXK = 32

        def _maxk(x, k):
            _, idx = jax.lax.top_k(x, k)
            rows = jnp.arange(x.shape[0])[:, None]
            mask = jnp.zeros_like(x).at[rows, idx].set(1.0)
            return x * mask
        n = feat.shape[0]
        h_self = feat @ W_self
        h_neigh = feat @ W_neigh
        h_sparse = _maxk(h_neigh, MAXK)
        msg = h_sparse[src]
        summed = jax.ops.segment_sum(msg, dst, num_segments=n)
        deg = jax.ops.segment_sum(jnp.ones((src.shape[0],), dtype=feat.dtype), dst, num_segments=n)
        neigh = summed / jnp.maximum(deg, 1.0)[:, None]
        return h_self + neigh

    def _L0_ffn_ref(x, W_fx, b_fx, W_x, b_x, W_slice, b_slice, W_q, W_k, W_v, W_out, b_out, temperature):
        import jax, jax.numpy as jnp
        import numpy as np
        DIM = 256
        H = 8
        D = 64
        G = 64
        INNER = H * D
        SCALE = D ** (-0.5)
        B, N, _ = x.shape
        fx_mid = (x @ W_fx + b_fx).reshape(B, N, H, D).transpose(0, 2, 1, 3)
        x_mid = (x @ W_x + b_x).reshape(B, N, H, D).transpose(0, 2, 1, 3)
        temp = jnp.clip(temperature, 0.1, 5.0)
        slice_weights = jax.nn.softmax((x_mid @ W_slice + b_slice) / temp, axis=-1)
        slice_norm = slice_weights.sum(axis=2)
        slice_token = jnp.einsum('bhnc,bhng->bhgc', fx_mid, slice_weights)
        slice_token = slice_token / (slice_norm[..., None] + 1e-05)
        q = slice_token @ W_q
        k = slice_token @ W_k
        v = slice_token @ W_v
        attn = jax.nn.softmax(jnp.einsum('bhgc,bhkc->bhgk', q, k) * SCALE, axis=-1)
        out_slice = jnp.einsum('bhgk,bhkc->bhgc', attn, v)
        out_x = jnp.einsum('bhgc,bhng->bhnc', out_slice, slice_weights)
        out_x = out_x.transpose(0, 2, 1, 3).reshape(B, N, INNER)
        return out_x @ W_out + b_out
    x = x + _L0_gnn_ref(_layernorm(x, axis=-1), L0_gnn_W_self, L0_gnn_W_neigh, src, dst)
    x = x + _L0_ffn_ref(_layernorm(x, axis=-1)[None], L0_ffn_W_fx, L0_ffn_b_fx, L0_ffn_W_x, L0_ffn_b_x, L0_ffn_W_slice, L0_ffn_b_slice, L0_ffn_W_q, L0_ffn_W_k, L0_ffn_W_v, L0_ffn_W_out, L0_ffn_b_out, L0_ffn_temperature)[0]
    return x

_drawn_inputs = setup_inputs


def setup_inputs(seed=0):
    import zlib

    import numpy as np

    out = dict(_drawn_inputs(seed))
    spreads = {'L0_ffn_b_fx': (0.0, 0.1),
     'L0_ffn_b_x': (0.0, 0.8),
     'L0_ffn_b_slice': (0.0, 0.8),
     'L0_ffn_b_out': (0.0, 0.1),
     'L0_ffn_temperature': (0.5, 0.6)}
    factors = {'L0_ffn_W_fx': 4.101,
     'L0_ffn_W_x': 8.0,
     'L0_ffn_W_slice': 8.0,
     'L0_ffn_W_q': 8.0,
     'L0_ffn_W_k': 8.0}
    for name, (base, spread) in spreads.items():
        noise = np.random.default_rng([zlib.crc32(name.encode()), seed]).standard_normal(out[name].shape)
        drawn = base * np.exp(spread * noise) if base else spread * noise
        out[name] = jnp.asarray(drawn.astype(out[name].dtype))
    for name, factor in factors.items():
        out[name] = (out[name] * factor).astype(out[name].dtype)
    return out
```

```python
from contextlib import ExitStack

import concourse.bass as bass
import numpy as np
from concourse import mybir

P = 128
N = 12500
D = 256
E = 200000
TOPK = 32
H = 8
DH = 64
G = 64
HG = H * G
TN = -(-N // P)
LAST = N - (TN - 1) * P
TE = -(-E // P)
CH = -(-TE // P)
FULL_E = E // P
LEFT_E = E - FULL_E * P
FULL_CH = FULL_E // P
LEFT_CH = FULL_E - FULL_CH * P
RING = 16
AHEAD = 32
EPS = 1e-5
TAKEN = -3.0e38
FAR = float(1 << 20)
MAXE = 4096.0
XCH = 14


class Tile:

    def __init__(self, k, step, at):
        self.k, self.step, self.at = k, step, at
        self.i = at if isinstance(k, int) else k * step + at

    def back(self, d):
        return Tile(self.k, self.step, self.at - d)

    def exists(self):
        return not isinstance(self.k, int) or 0 <= self.at < TN

    def is_first(self):
        return isinstance(self.k, int) and self.at == 0

    def is_last(self):
        return isinstance(self.k, int) and self.at == TN - 1

    def slot(self, m):
        return self.at % m

    def round(self, m):
        return self.at // m if isinstance(self.k, int) else self.k * (self.step // m) + self.at // m


def sweep(eng, first, loop_from, loop_to, last, unroll, body):
    for t in range(first, loop_from):
        body(Tile(0, 0, t))
    with eng.Fori(0, (loop_to - loop_from) // unroll) as k:
        for u in range(unroll):
            body(Tile(k, unroll, loop_from + u))
    for t in range(loop_to, last + 1):
        body(Tile(0, 0, t))


def wait(eng, sem, count):
    if not (isinstance(count, int) and count <= 0):
        eng.wait_ge(sem, count)


def build(nc, x, src, dst, w_self, w_neigh, w_fx, b_fx, w_x, b_x, w_slice, b_slice, w_q, w_k, w_v, w_out, b_out,
          temperature, out):
    f32, bf16, i32 = mybir.dt.float32, mybir.dt.bfloat16, mybir.dt.int32
    ALU, ACT, AX = mybir.AluOpType, mybir.ActivationFunctionType, mybir.AxisListType

    messages = nc.dram_tensor("messages", [TN * P, 3 * D], bf16, kind="Internal").ap()
    weights_t = nc.dram_tensor("weights_t", [TN, P, HG], f32, kind="Internal").ap()
    plan_dram = nc.dram_tensor("plan_dram", [TN + 1, 4], i32, kind="Internal").ap()

    whole = ExitStack()

    def keeper(stack):
        return (lambda name, shape, dt: stack.enter_context(nc.sbuf_tensor(name, shape, dt)),
                lambda name: stack.enter_context(nc.psum_tensor(name, [P, 512], f32)),
                lambda name: stack.enter_context(nc.semaphore(name)))

    sb, _, _ = keeper(whole)
    x_all = sb("x_all", [P, TN, D], f32)
    src_cols = sb("src_cols", [P, CH * P], f32)
    dst_cols = sb("dst_cols", [P, CH * P], f32)
    plan = sb("plan", [1, (TN + 1) * 4], i32)
    window = sb("window", [P, TN + 1], f32)
    minus_window = sb("minus_window", [P, TN + 1], f32)
    node_row = sb("node_row", [P, P], bf16)
    ident = sb("ident", [P, P], f32)
    ones = sb("ones", [P, P], f32)
    w_logit = sb("w_logit", [P, 2, HG], f32)
    b_logit = sb("b_logit", [P, HG], f32)
    token_sum = sb("token_sum", [P, 2, HG], f32)
    norm_sum = sb("norm_sum", [P, HG], f32)

    def x_tile(t):
        return x_all[:, bass.ds(t.i, 1), :].rearrange("p o d -> p (o d)")

    with ExitStack() as one:
        sb, pb, sem = keeper(one)
        src_int = sb("src_int", [P, CH, P], i32)
        dst_int = sb("dst_int", [P, CH, P], i32)
        src_f = src_int[:, :, :].bitcast(f32)
        dst_f = dst_int[:, :, :].bitcast(f32)
        tail_f = sb("tail_f", [P, P], f32)
        node_int = sb("node_int", [P, P], i32)
        win_int = sb("win_int", [P, TN + 1], i32)
        edge_int = sb("edge_int", [P, CH], i32)
        edge_no = sb("edge_no", [P, CH], f32)
        dmin = sb("dmin", [P, CH], f32)
        dmax = sb("dmax", [P, CH], f32)
        starts = sb("starts", [P, TN, CH], f32)
        needed = sb("needed", [P, TN, CH], f32)
        last_part = sb("last_part", [P, TN], f32)
        first_part = sb("first_part", [P, TN], f32)
        earlier = sb("earlier", [P, P], f32)
        plan_f = sb("plan_f", [P, 4], f32)
        cols = sb("cols", [P, 8], f32)
        plan_i = sb("plan_i", [P, 4], i32)
        w_both = sb("w_both", [P, 2, 2 * D], f32)
        wx = sb("wx", [P, 2, HG], f32)
        wx_t = sb("wx_t", [P, 4, D], f32)
        ws_pair = sb("ws_pair", [P, P], f32)
        bx_cols = sb("bx_cols", [P, 4], f32)
        bx_wide = sb("bx_wide", [P, 4, P], f32)
        bs_row = sb("bs_row", [P, G], f32)
        temp = sb("temp", [P, H], f32)
        rtemp = sb("rtemp", [P, H], f32)
        stats = sb("stats", [P, 2, 6], f32)
        mv = sb("mv", [P, 2, 2], f32)
        eps = sb("eps", [P, 1], f32)
        std = sb("std", [P, 2], f32)
        rstd = sb("rstd", [P, 2], f32)
        shift = sb("shift", [P, 2], f32)
        xn = sb("xn", [P, 2, D], f32)
        xn_t = sb("xn_t", [P, 2, 2, P], f32)
        neigh = sb("neigh", [P, 2, D], f32)
        left = sb("left", [P, D], f32)
        top8 = sb("top8", [P, 4, 8], f32)
        sparse = sb("sparse", [P, 2, D], f32)
        rest = sb("rest", [P, 2, D], f32)
        parts = sb("parts", [P, 2, 3 * D], bf16)
        ps_t = [pb("ps_t0"), pb("ps_t1")]
        ps_h = [pb("ps_h0"), pb("ps_h1")]
        ps_p = [pb("ps_p0"), pb("ps_p1")]
        ps_w = [pb("ps_w0"), pb("ps_w1")]

        pads_set, edges_in, weights_in, x_in = sem("pads_set"), sem("edges_in"), sem("weights_in"), sem("x_in")
        tables_made, consts_made, prep, prep_pe, prep_act = (
            sem("tables_made"), sem("consts_made"), sem("prep"), sem("prep_pe"), sem("prep_act"))
        plan_out, plan_in = sem("plan_out"), sem("plan_in")
        stats_made, means_made, std_made, rstd_made, shift_made = (
            sem("stats_made"), sem("means_made"), sem("std_made"), sem("rstd_made"), sem("shift_made"))
        xn_done, xt_done, xt_kept, h_done, neigh_kept, base_done, top_step, sparse_done = (
            sem("xn_done"), sem("xt_done"), sem("xt_kept"), sem("h_done"), sem("neigh_kept"),
            sem("base_done"), sem("top_step"), sem("sparse_done"))
        part1, rest1, part2, part3 = sem("part1"), sem("rest1"), sem("part2"), sem("part3")
        stored = [sem("stored0"), sem("stored1")]
        FIRST, LOOP, LOOP_END, END = -3, 3, TN - 3, TN
        TOPS = 8
        block = one.enter_context(nc.Block())

        @block.sync
        def _(sp):
            sp.wait_ge(pads_set, 3)
            for rows, ints in ((dst, dst_int), (src, src_int)):
                sp.dma_start(ints[:, 0:FULL_CH, :],
                             rows[0:FULL_CH * P * P].rearrange("(c p n) -> p c n", p=P, n=P)).then_inc(edges_in, 16)
                sp.dma_start(ints[0:LEFT_CH, FULL_CH, :],
                             rows[FULL_CH * P * P:FULL_E * P].rearrange("(p n) -> p n", n=P)).then_inc(edges_in, 16)
                sp.dma_start(ints[LEFT_CH:LEFT_CH + 1, FULL_CH, 0:LEFT_E],
                             rows[FULL_E * P:E].rearrange("(p n) -> p n", p=1)).then_inc(edges_in, 16)
            sp.dma_start(wx[:, :, :], w_x.rearrange("(c p) n -> p c n", p=P)).then_inc(weights_in, 16)
            sp.dma_start(ws_pair[0:G, 0:G], w_slice).then_inc(weights_in, 16)
            sp.dma_start(ws_pair[G:P, G:P], w_slice).then_inc(weights_in, 16)
            with nc.allow_non_contiguous_dma(reason="512 single values, once"):
                sp.dma_start(bx_cols[:, :], b_x.rearrange("(c p) -> p c", p=P)).then_inc(weights_in, 16)
            sp.dma_start(bs_row[:, :], b_slice.rearrange("(o n) -> o n", o=1).broadcast_to([P, G])).then_inc(weights_in, 16)
            sp.dma_start(temp[:, :], temperature.rearrange("a h b c -> a (h b c)").broadcast_to([P, H])).then_inc(weights_in, 16)
            sp.dma_start(w_both[:, :, 0:D], w_self.rearrange("(c p) n -> p c n", p=P)).then_inc(weights_in, 16)
            sp.dma_start(w_both[:, :, D:2 * D], w_neigh.rearrange("(c p) n -> p c n", p=P)).then_inc(weights_in, 16)
            for a in range(0, TN - 1, XCH):
                b = min(a + XCH, TN - 1)
                sp.dma_start(x_all[:, a:b, :], x[a * P:b * P, :].rearrange("(t p) d -> p t d", p=P)).then_inc(x_in, 16)
            sp.dma_start(x_all[0:LAST, TN - 1, :], x[(TN - 1) * P:N, :]).then_inc(x_in, 16)
            sp.wait_ge(prep, 25)
            sp.dma_start(plan_dram, plan_i[0:TN + 1, :]).then_inc(plan_out, 16)
            sp.wait_ge(plan_out, 16)
            sp.dma_start(plan[:, :], plan_dram.rearrange("t f -> (t f)").rearrange("(o n) -> o n", o=1)).then_inc(plan_in, 16)

            def store(t):
                sp.wait_ge(part3, t.i + 1)
                sp.dma_start(messages[bass.ds(t.i * P, P), :], parts[:, t.slot(2), :]).then_inc(stored[t.slot(2)], 16)
            sweep(sp, 0, 0, TN, TN - 1, 2, store)
            sp.wait_ge(plan_in, 16)
            for s in stored:
                sp.wait_ge(s, 16 * (TN // 2))

        @block.gpsimd
        def _(pool):
            nc.gpsimd.iota(win_int[:, :], pattern=[[P, TN + 1]], base=0, channel_multiplier=0).then_inc(tables_made, 1)
            nc.gpsimd.iota(edge_int[:, :], pattern=[[P, CH]], base=1, channel_multiplier=1).then_inc(tables_made, 1)
            nc.gpsimd.iota(node_int[:, :], pattern=[[1, P]], base=0, channel_multiplier=0).then_inc(tables_made, 1)
            pool.wait_ge(consts_made, 3)
            nc.gpsimd.affine_select(out=ident[:, :], in_=ident[:, :], compare_op=ALU.not_equal, fill=1.0, base=0,
                                    pattern=[[-1, P]], channel_multiplier=1).then_inc(tables_made, 1)
            nc.gpsimd.affine_select(out=earlier[:, :], in_=earlier[:, :], compare_op=ALU.is_ge, fill=1.0, base=0,
                                    pattern=[[-1, P]], channel_multiplier=1).then_inc(tables_made, 1)

            def split(it):
                t = it.back(1)
                if not t.exists():
                    return
                s = t.slot(2)
                pool.wait_ge(part1, t.i + 1)
                wait(pool, part3, t.i - 1)
                nc.gpsimd.tensor_tensor(rest[:, s, :], sparse[:, s, :], parts[:, s, 0:D], ALU.subtract).then_inc(rest1, 1)
                pool.wait_ge(part2, t.i + 1)
                nc.gpsimd.tensor_tensor(parts[:, s, 2 * D:3 * D], rest[:, s, :], parts[:, s, D:2 * D],
                                        ALU.subtract).then_inc(part3, 1)
            sweep(pool, FIRST, LOOP, LOOP_END, END, 2, split)

        @block.scalar
        def _(act):
            nc.scalar.preload_act_table(ACT.Sqrt)
            for n in range(8):
                full = n % 4 < 3
                cols_of = src_cols if n < 4 else dst_cols
                width = 4 * P if full else (CH - 12) * P
                act.wait_ge(prep_pe, n + 1)
                nc.scalar.copy(cols_of[:, (n % 4) * 4 * P:(n % 4) * 4 * P + width],
                               ps_t[n % 2][:, 0:width]).then_inc(prep_act, 1)
            act.wait_ge(prep_pe, 9)
            nc.scalar.copy(wx_t[:, 0:2, :], ps_w[0][:, :].rearrange("p (a k) -> p a k", a=2)).then_inc(prep_act, 1)
            act.wait_ge(prep_pe, 10)
            nc.scalar.copy(wx_t[:, 2:4, :], ps_w[1][:, :].rearrange("p (a k) -> p a k", a=2)).then_inc(prep_act, 1)

            act.wait_ge(consts_made, 4)

            def step(it):
                t = it.back(-3)
                if t.exists():
                    s = t.slot(2)
                    act.wait_ge(means_made, t.i + 1)
                    wait(act, rstd_made, t.i - 1)
                    nc.scalar.activation(std[:, s:s + 1], mv[:, s, 1:2], ACT.Sqrt, bias=eps[:, :]).then_inc(std_made, 1)
                t = it.back(-2)
                if t.exists():
                    s = t.slot(2)
                    act.wait_ge(shift_made, t.i + 1)
                    wait(act, xt_done, t.i - 1)
                    nc.scalar.activation(xn[:, s, :], x_tile(t), ACT.Identity, bias=shift[:, s:s + 1],
                                         scale=rstd[:, s:s + 1]).then_inc(xn_done, 1)
                    act.wait_ge(xt_done, t.i + 1)
                    wait(act, h_done, t.i - 1)
                    nc.scalar.copy(xn_t[:, s, :, :].rearrange("p a b -> p (a b)"), ps_t[s][:, 0:D]).then_inc(xt_kept, 1)
                t = it.back(1)
                if t.exists():
                    s = t.slot(2)
                    act.wait_ge(sparse_done, t.i + 1)
                    wait(act, stored[s], t.round(2) * 16)
                    nc.scalar.copy(parts[:, s, 0:D], sparse[:, s, :]).then_inc(part1, 1)
                t = it.back(-1)
                if t.exists():
                    s = t.slot(2)
                    act.wait_ge(h_done, t.i + 1)
                    wait(act, sparse_done, t.i - 1)
                    nc.scalar.copy(neigh[:, s, :], ps_h[s][:, D:2 * D]).then_inc(neigh_kept, 1)
                t = it.back(1)
                if t.exists():
                    s = t.slot(2)
                    act.wait_ge(rest1, t.i + 1)
                    nc.scalar.copy(parts[:, s, D:2 * D], rest[:, s, :]).then_inc(part2, 1)
            sweep(act, FIRST, LOOP, LOOP_END, END, 2, step)

        @block.vector
        def _(dve):
            nc.vector.memset(dst_int[:, FULL_CH, :], -1).then_inc(pads_set, 1)
            nc.vector.memset(src_int[:, FULL_CH, :], 0).then_inc(pads_set, 1)
            nc.vector.memset(x_all[:, TN - 1, :], 0.0)
            nc.vector.memset(ws_pair[:, :], 0.0).then_inc(pads_set, 1)
            nc.vector.memset(ident[:, :], 0.0).then_inc(consts_made, 1)
            nc.vector.memset(earlier[:, :], 0.0).then_inc(consts_made, 1)
            nc.vector.memset(ones[:, :], 1.0).then_inc(consts_made, 1)
            nc.vector.memset(eps[:, :], EPS).then_inc(consts_made, 1)
            nc.vector.memset(plan_f[:, :], 1.0)
            dve.wait_ge(tables_made, 3)
            nc.vector.tensor_copy(window[:, :], win_int[:, :])
            nc.vector.tensor_scalar(minus_window[:, :], win_int[:, :], -1.0, None, ALU.mult)
            nc.vector.tensor_copy(edge_no[:, :], edge_int[:, :])
            nc.vector.tensor_copy(node_row[:, :], node_int[:, :])
            dve.wait_ge(edges_in, 96)
            nc.vector.tensor_copy(src_f, src_int[:, :, :]).then_inc(prep, 1)
            nc.vector.tensor_copy(dst_f, dst_int[:, :, :]).then_inc(prep, 1)
            dve.wait_ge(prep, 2)
            nc.vector.tensor_reduce(dmax[:, :], dst_f, AX.X, ALU.max).then_inc(prep, 1)
            nc.vector.tensor_reduce(dmin[:, 0:FULL_CH], dst_f[:, 0:FULL_CH, :], AX.X, ALU.min).then_inc(prep, 1)
            nc.vector.tensor_scalar(tail_f[:, :], dst_f[:, FULL_CH, :], 0.0, FAR, ALU.is_lt, ALU.mult).then_inc(prep, 1)
            dve.wait_ge(prep, 5)
            nc.vector.tensor_tensor(tail_f[:, :], tail_f[:, :], dst_f[:, FULL_CH, :], ALU.add).then_inc(prep, 1)
            dve.wait_ge(prep, 6)
            nc.vector.tensor_reduce(dmin[:, FULL_CH:CH], tail_f[:, :], AX.X, ALU.min).then_inc(prep, 1)
            dve.wait_ge(prep, 7)
            shape = [P, TN, CH]

            def per_edge_tile(a):
                return a[:, :].rearrange("p (o c) -> p o c", o=1).broadcast_to(shape)

            def per_node_tile(a, at):
                return a[:, at:at + TN].rearrange("p (t o) -> p t o", o=1).broadcast_to(shape)
            nc.vector.tensor_tensor(starts[:, :, :], per_edge_tile(dmin), per_node_tile(window, 1), ALU.is_lt).then_inc(prep, 1)
            nc.vector.tensor_tensor(needed[:, :, :], per_edge_tile(dmax), per_node_tile(window, 0), ALU.is_ge).then_inc(prep, 1)
            dve.wait_ge(prep, 9)
            nc.vector.tensor_tensor(needed[:, :, :], needed[:, :, :], starts[:, :, :], ALU.mult).then_inc(prep, 1)
            dve.wait_ge(prep, 10)
            nc.vector.tensor_tensor(starts[:, :, :], needed[:, :, :], per_edge_tile(edge_no), ALU.mult).then_inc(prep, 1)
            dve.wait_ge(prep, 11)
            nc.vector.tensor_reduce(last_part[:, :], starts[:, :, :], AX.X, ALU.max).then_inc(prep, 1)
            nc.vector.tensor_scalar(edge_no[:, :], edge_no[:, :], -1.0, MAXE, ALU.mult, ALU.add).then_inc(prep, 1)
            dve.wait_ge(prep, 13)
            nc.vector.tensor_tensor(needed[:, :, :], needed[:, :, :], per_edge_tile(edge_no), ALU.mult).then_inc(prep, 1)
            dve.wait_ge(prep, 14)
            nc.vector.tensor_reduce(first_part[:, :], needed[:, :, :], AX.X, ALU.max).then_inc(prep, 1)
            dve.wait_ge(prep_pe, 11)
            nc.vector.tensor_reduce(cols[0:TN, 0:2], ps_p[0][0:TN, 0:2 * P].rearrange("t (a p) -> t a p", a=2), AX.X,
                                    ALU.max).then_inc(prep, 1)
            dve.wait_ge(prep, 16)
            nc.vector.tensor_scalar(cols[0:TN, 2:3], cols[0:TN, 0:1], 1.0, None, ALU.min).then_inc(prep, 1)
            nc.vector.tensor_scalar(cols[0:TN, 3:4], cols[0:TN, 1:2], -1.0, MAXE - 1.0, ALU.mult, ALU.add).then_inc(prep, 1)
            dve.wait_ge(prep, 18)
            nc.vector.tensor_tensor(plan_f[0:TN, 0:1], cols[0:TN, 2:3], cols[0:TN, 3:4], ALU.mult).then_inc(prep, 1)
            dve.wait_ge(prep, 19)
            nc.vector.tensor_tensor(cols[0:TN, 4:5], cols[0:TN, 0:1], plan_f[0:TN, 0:1], ALU.subtract).then_inc(prep, 1)
            dve.wait_ge(prep, 20)
            nc.vector.tensor_scalar(plan_f[0:TN, 1:2], cols[0:TN, 4:5], 1.0, None, ALU.max).then_inc(prep, 1)
            dve.wait_ge(prep_pe, 12)
            nc.vector.tensor_copy(plan_f[0:TN + 1, 2:3], ps_p[1][0:TN + 1, 0:1]).then_inc(prep, 1)
            nc.vector.tensor_scalar(plan_f[0:TN + 1, 3:4], ps_p[1][0:TN + 1, 0:1], -1.0, None,
                                    ALU.add).then_inc(prep, 1)
            dve.wait_ge(prep, 23)
            nc.vector.tensor_copy(plan_i[0:TN + 1, :], plan_f[0:TN + 1, :]).then_inc(prep, 1)
            dve.wait_ge(prep, 24)
            nc.vector.tensor_scalar(plan_i[0:TN + 1, 3:4], plan_i[0:TN + 1, 3:4], AHEAD.bit_length() - 1, None,
                                    ALU.arith_shift_right).then_inc(prep, 1)
            dve.wait_ge(weights_in, 128)
            nc.vector.tensor_scalar(temp[:, :], temp[:, :], 0.1, 5.0, ALU.max, ALU.min).then_inc(prep, 1)
            nc.vector.tensor_copy(bx_wide[:, :, :],
                                  bx_cols[:, :].rearrange("p (c o) -> p c o", o=1).broadcast_to([P, 4, P])).then_inc(prep, 1)
            dve.wait_ge(prep, 27)
            nc.vector.reciprocal(rtemp[:, :], temp[:, :]).then_inc(prep, 1)
            dve.wait_ge(prep, 28)
            by_head = rtemp[:, :].rearrange("p (h o) -> p h o", o=1).broadcast_to([P, H, G])
            for c in range(2):
                dve.wait_ge(prep_pe, 13 + c)
                nc.vector.tensor_tensor(w_logit[:, c, :].rearrange("p (h g) -> p h g", h=H),
                                        ps_w[c][:, :].rearrange("p (h g) -> p h g", h=H), by_head,
                                        ALU.mult).then_inc(prep, 1)
            dve.wait_ge(prep_pe, 15)
            b_heads = b_logit[:, :].rearrange("p (h g) -> p h g", h=H)
            nc.vector.tensor_tensor(b_heads, ps_p[0][:, :].rearrange("p (h g) -> p h g", h=H),
                                    bs_row[:, :].rearrange("p (o g) -> p o g", o=1).broadcast_to([P, H, G]),
                                    ALU.add).then_inc(prep, 1)
            dve.wait_ge(prep, 31)
            nc.vector.tensor_tensor(b_heads, b_heads, by_head, ALU.mult).then_inc(prep, 1)
            dve.wait_ge(x_in, 16 * (-(-(TN - 1) // XCH) + 1))

            def means(t):
                s = t.slot(2)
                nc.vector.bn_stats(stats[:, s, :], x_tile(t)).then_inc(stats_made, 1)
                dve.wait_ge(stats_made, t.i + 1)
                wait(dve, std_made, t.i - 1)
                dve.nop(nofuse=True)
                nc.vector.bn_aggr(mv[:, s, :], stats[:, s, :]).then_inc(means_made, 1)

            def shifts(t):
                s = t.slot(2)
                dve.wait_ge(std_made, t.i + 1)
                wait(dve, xn_done, t.i - 1)
                nc.vector.reciprocal(rstd[:, s:s + 1], std[:, s:s + 1]).then_inc(rstd_made, 1)
                dve.wait_ge(rstd_made, t.i + 1)
                nc.vector.tensor_scalar(shift[:, s:s + 1], mv[:, s, 0:1], rstd[:, s:s + 1], -1.0, ALU.mult,
                                        ALU.mult).then_inc(shift_made, 1)

            def top(t):
                s, done = t.slot(2), t.i * TOPS
                dve.wait_ge(neigh_kept, t.i + 1)
                nc.vector.tensor_tensor(x_tile(t), x_tile(t), ps_h[s][:, 0:D], ALU.add).then_inc(base_done, 1)
                for r in range(TOPK // 8):
                    seen = neigh[:, s, :] if r == 0 else left[:, :]
                    if r == 0:
                        wait(dve, sparse_done, t.i)
                    else:
                        dve.wait_ge(top_step, done + 2 * r)
                    dve.nop(nofuse=True)
                    nc.vector.max(top8[:, r, :], seen).then_inc(top_step, 1)
                    dve.wait_ge(top_step, done + 2 * r + 1)
                    dve.nop(nofuse=True)
                    nc.vector.match_replace(left[:, :], top8[:, r, :], seen, TAKEN).then_inc(top_step, 1)
                dve.wait_ge(top_step, done + TOPS)
                wait(dve, rest1, t.i - 1)
                nc.vector.scalar_tensor_tensor(sparse[:, s, :], left[:, :], TAKEN, neigh[:, s, :], ALU.is_equal,
                                               ALU.mult).then_inc(sparse_done, 1)

            def step(it):
                if it.back(-3).exists():
                    means(it.back(-3))
                if it.back(-2).exists():
                    shifts(it.back(-2))
                if it.exists():
                    top(it)
            sweep(dve, FIRST, LOOP, LOOP_END, END, 2, step)

        @block.tensor
        def _(pe):
            pe.wait_ge(tables_made, 5)
            pe.wait_ge(prep, 2)
            for n in range(8):
                rows = src_f if n < 4 else dst_f
                chunks = range((n % 4) * 4, min((n % 4) * 4 + 4, CH))
                wait(pe, prep_act, n - 1)
                for c in chunks:
                    done = nc.tensor.transpose(ps_t[n % 2][:, (c % 4) * P:(c % 4 + 1) * P], rows[:, c, :], ident[:, :])
                done.then_inc(prep_pe, 1)
            pe.wait_ge(weights_in, 128)
            for n in range(2):
                for c in range(2):
                    for k in range(2):
                        at = (2 * c + k) * P
                        done = nc.tensor.transpose(ps_w[n][:, at:at + P], wx[:, k, (2 * n + c) * P:(2 * n + c + 1) * P],
                                                   ident[:, :])
                done.then_inc(prep_pe, 1)
            pe.wait_ge(prep, 15)
            nc.tensor.transpose(ps_p[0][0:TN, 0:P], last_part[:, :], ident[:, :])
            nc.tensor.transpose(ps_p[0][0:TN, P:2 * P], first_part[:, :], ident[:, :]).then_inc(prep_pe, 1)
            pe.wait_ge(prep, 21)
            nc.tensor.matmul(ps_p[1][0:TN + 1, 0:1], earlier[0:TN, 0:TN + 1], plan_f[0:TN, 1:2], start=True,
                             stop=True).then_inc(prep_pe, 1)
            pe.wait_ge(prep_act, 10)
            for k in range(2):
                for n in range(4):
                    done = nc.tensor.matmul(ps_w[k][:, n * P:(n + 1) * P], wx_t[:, n, k * P:(k + 1) * P], ws_pair[:, :],
                                            start=True, stop=True)
                done.then_inc(prep_pe, 1)
            pe.wait_ge(prep, 27)
            for n in range(4):
                done = nc.tensor.matmul(ps_p[0][:, n * P:(n + 1) * P], bx_wide[:, n, :], ws_pair[:, :], start=True, stop=True)
            done.then_inc(prep_pe, 1)

            def step(it):
                t = it.back(-2)
                if t.exists():
                    s = t.slot(2)
                    pe.wait_ge(xn_done, t.i + 1)
                    wait(pe, xt_kept, t.i - 1)
                    if t.is_first():
                        pe.wait_ge(prep_act, 8)
                    nc.tensor.transpose(ps_t[s][:, 0:P], xn[:, s, 0:P], ident[:, :])
                    nc.tensor.transpose(ps_t[s][:, P:D], xn[:, s, P:D], ident[:, :]).then_inc(xt_done, 1)
                t = it.back(-1)
                if t.exists():
                    s = t.slot(2)
                    pe.wait_ge(xt_kept, t.i + 1)
                    wait(pe, neigh_kept, t.i - 1)
                    wait(pe, base_done, t.i - 1)
                    nc.tensor.matmul(ps_h[s][:, :], xn_t[:, s, 0, :], w_both[:, 0, :], start=True, stop=False)
                    nc.tensor.matmul(ps_h[s][:, :], xn_t[:, s, 1, :], w_both[:, 1, :], start=False, stop=True).then_inc(h_done, 1)
            sweep(pe, FIRST, LOOP, LOOP_END, END, 2, step)

    with ExitStack() as two:
        sb, pb, sem = keeper(two)
        index = sb("index", [P, AHEAD], i32)
        onehot = sb("onehot", [P, AHEAD, P], bf16)
        gathered = sb("gathered", [P, RING, 3 * D + 2], bf16)
        zeros = sb("zeros", [P, D + 1], bf16)
        rdeg = sb("rdeg", [P, 2, 2], f32)
        stats = sb("stats2", [P, 6], f32)
        mv = sb("mv2", [P, 2], f32)
        spread = sb("spread", [P, 1], f32)
        rough = sb("rough", [P, 2], f32)
        error = sb("error", [P, 1], f32)
        rstd = sb("rstd2", [P, 1], f32)
        xn = sb("xn2", [P, 4, D], f32)
        xn_t = sb("xn_t2", [P, 2, 2, P], f32)
        logits = sb("logits", [P, 2, HG], f32)
        peak = sb("peak", [P, H], f32)
        weights = sb("weights", [P, 2, HG], f32)
        total = sb("total", [P, 2, H], f32)
        turned = sb("turned", [P, 2, HG], f32)
        ps_sum = [pb("ps_sum0"), pb("ps_sum1")]
        ps_x, ps_l, ps_s = pb("ps_x"), pb("ps_l"), pb("ps_s")
        ps_tok = [pb("ps_tok0"), pb("ps_tok1")]
        ps_norm = pb("ps_norm")

        consts_made = sem("consts_made2")
        landed = [sem(f"landed{j}") for j in range(RING)]
        index_ready, onehot_ready, messages_in, used = sem("index_ready"), sem("onehot_ready"), sem("messages_in"), sem("used")
        summed, add_step, mean_added, xn_ready, xt_done, xt_kept, l_done, l_kept, l_step, l_ready = (
            sem("summed"), sem("add_step"), sem("mean_added"), sem("xn_ready"), sem("xt_done2"), sem("xt_kept2"),
            sem("l_done"), sem("l_kept"), sem("l_step"), sem("l_ready"))
        rough_made = sem("rough_made")
        exp_done, w_step, w_ready, tokens_done, turned_kept, sums_kept = (
            sem("exp_done"), sem("w_step"), sem("w_ready"), sem("tokens_done"), sem("turned_kept"), sem("sums_kept"))
        stored = [sem("w_stored0"), sem("w_stored1")]
        ADDS, WAYS = 8, 2
        LOOP, LOOP_END, END = 7, TN - 3, TN + 4
        STEPS_MAX = TE * TN

        def planned(eng, t, field, most):
            at = bass.ds(t.i * 4 + field, 1) if isinstance(t, Tile) else slice(t * 4 + field, t * 4 + field + 1)
            return eng.value_load(plan[0:1, at], min_val=0, max_val=most)

        def edge_column(first, i):
            return bass.ds(nc.s_assert_within(first + i, 0, TE - 1,
                                              skip_runtime_bounds_check_because="the plan names edge tiles that exist"), 1)

        block = two.enter_context(nc.Block())

        @block.sync
        def _(sp):
            rounds = planned(sp, TN, 3, STEPS_MAX) + 1
            with sp.Fori(0, rounds) as k:
                for j in range(AHEAD):
                    sp.wait_ge(landed[j % RING], k * (16 * AHEAD // RING) + 16 * (j // RING + 1))
                    sp.sem_inc(messages_in, 1)

        @block.gpsimd
        def _(pool):
            rounds = planned(pool, TN, 3, STEPS_MAX) + 1
            with pool.Fori(0, rounds) as k:
                for j in range(AHEAD):
                    pool.wait_ge(index_ready, k * AHEAD + (j + 1))
                    pool.wait_ge(used, k * AHEAD + (j + 1 + AHEAD - RING))
                    pool.nop(nofuse=True)
                    nc.gpsimd.indirect_dma_start(
                        gathered[:, j % RING, 0:3 * D], None, messages,
                        bass.IndirectOffsetOnAxis(ap=index[:, j:j + 1], axis=0)).then_inc(landed[j % RING], 16)

        @block.scalar
        def _(act):
            nc.scalar.preload_act_table_set("natural_log_exp_and_others")

            def indices(t):
                first, steps, before = (planned(act, t, f, m) for f, m in ((0, TE - 1), (1, TE), (2, STEPS_MAX)))
                with act.Fori(0, steps) as i:
                    s = act.snap(before + i)
                    act.wait_ge(used, s + 1)
                    nc.scalar.copy(index[:, bass.ds(s % AHEAD, 1)], src_cols[:, edge_column(first, i)]).then_inc(index_ready, 1)

            def step(it):
                if it.exists():
                    indices(it)
                t = it.back(1)
                if t.exists():
                    act.wait_ge(add_step, t.i * ADDS + 5)
                    nc.scalar.activation(rough[:, 0:1], spread[:, :], ACT.Ln).then_inc(rough_made, 1)
                    act.wait_ge(rough_made, t.i * 2 + 1)
                    nc.scalar.activation(rough[:, 1:2], rough[:, 0:1], ACT.Exp, scale=-0.5).then_inc(rough_made, 1)
                t = it.back(2)
                if t.exists():
                    s = t.slot(2)
                    act.wait_ge(xt_done, t.i + 1)
                    wait(act, l_done, t.i - 1)
                    nc.scalar.copy(xn_t[:, s, :, :].rearrange("p a b -> p (a b)"), ps_x[:, 0:D]).then_inc(xt_kept, 1)
                t = it.back(4)
                if t.exists():
                    s = t.slot(2)
                    act.wait_ge(l_ready, t.i + 1)
                    wait(act, tokens_done, t.i - 1)
                    nc.scalar.activation(weights[:, s, :], logits[:, s, :], ACT.Exp).then_inc(exp_done, 1)
                t = it.back(5)
                if t.exists():
                    s = t.slot(2)
                    act.wait_ge(tokens_done, t.i + 1)
                    wait(act, stored[s], t.round(2) * 16)
                    nc.scalar.copy(turned[:, s, :], ps_s[:, :]).then_inc(turned_kept, 1)
                    act.wait_ge(turned_kept, t.i + 1)
                    act.dma_start(weights_t[bass.ds(t.i, 1), :, :].rearrange("o p n -> p (o n)"),
                                  turned[:, s, :]).then_inc(stored[s], 16)
            sweep(act, 0, LOOP, LOOP_END, END, 4, step)
            steps = planned(act, TN, 2, STEPS_MAX)
            act.wait_ge(index_ready, steps)
            act.nop(nofuse=True).then_inc(index_ready, AHEAD)
            for s in stored:
                act.wait_ge(s, 16 * (TN // 2))

        @block.vector
        def _(dve):
            nc.vector.memset(zeros[:, :], 0.0).then_inc(consts_made, 1)
            nc.vector.memset(gathered[:, :, 3 * D:3 * D + 1], 1.0).then_inc(consts_made, 1)

            def onehots(t):
                first, steps, before = (planned(dve, t, f, m) for f, m in ((0, TE - 1), (1, TE), (2, STEPS_MAX)))
                with dve.Fori(0, steps) as i:
                    s = dve.snap(before + i)
                    dve.wait_ge(used, s + 1)
                    nc.vector.tensor_scalar(
                        onehot[:, bass.ds(s % AHEAD, 1), :].rearrange("p o n -> p (o n)"), node_row[:, :],
                        dst_cols[:, edge_column(first, i)], minus_window[:, bass.ds(t.i, 1)], ALU.subtract,
                        ALU.is_equal).then_inc(onehot_ready, 1)

            def add_mean(t):
                s, done = t.slot(2), t.i * ADDS
                dve.wait_ge(summed, t.i + 1)
                nc.vector.tensor_scalar(rdeg[:, s, 0:1], ps_sum[s][:, D:D + 1], 1.0, None, ALU.max).then_inc(add_step, 1)
                dve.wait_ge(add_step, done + 1)
                nc.vector.reciprocal(rdeg[:, s, 1:2], rdeg[:, s, 0:1]).then_inc(add_step, 1)
                dve.wait_ge(add_step, done + 2)
                nc.vector.scalar_tensor_tensor(x_tile(t), ps_sum[s][:, 0:D], rdeg[:, s, 1:2], x_tile(t), ALU.mult,
                                               ALU.add).then_inc(mean_added, 1)
                dve.wait_ge(mean_added, t.i + 1)
                dve.nop(nofuse=True)
                nc.vector.bn_stats(stats[:, :], x_tile(t)).then_inc(add_step, 1)
                dve.wait_ge(add_step, done + 3)
                dve.nop(nofuse=True)
                nc.vector.bn_aggr(mv[:, :], stats[:, :]).then_inc(add_step, 1)
                dve.wait_ge(add_step, done + 4)
                nc.vector.tensor_scalar(spread[:, :], mv[:, 1:2], EPS, None, ALU.add).then_inc(add_step, 1)

            def norm(t):
                done = t.i * ADDS
                dve.wait_ge(rough_made, t.i * 2 + 2)
                nc.vector.scalar_tensor_tensor(error[:, :], rough[:, 1:2], rough[:, 1:2], spread[:, :], ALU.mult,
                                               ALU.mult).then_inc(add_step, 1)
                dve.wait_ge(add_step, done + 6)
                nc.vector.tensor_scalar(error[:, :], error[:, :], -0.5, 1.5, ALU.mult, ALU.add).then_inc(add_step, 1)
                dve.wait_ge(add_step, done + 7)
                nc.vector.tensor_tensor(rstd[:, :], rough[:, 1:2], error[:, :], ALU.mult).then_inc(add_step, 1)
                wait(dve, tokens_done, t.i - 3)
                dve.wait_ge(add_step, done + 8)
                nc.vector.tensor_scalar(xn[:, t.slot(4), :], x_tile(t), mv[:, 0:1], rstd[:, :], ALU.subtract,
                                        ALU.mult).then_inc(xn_ready, 1)

            def by_head(a):
                return a.rearrange("p (h g) -> p h g", h=H)

            def wide(a):
                return a.rearrange("p (h o) -> p h o", o=1).broadcast_to([a.shape[0], H, G])

            def less_peak(t):
                s = t.slot(2)
                dve.wait_ge(l_done, t.i + 1)
                wait(dve, exp_done, t.i - 1)
                nc.vector.tensor_tensor(logits[:, s, :], ps_l[:, :], b_logit[:, :], ALU.add).then_inc(l_kept, 1)
                dve.wait_ge(l_kept, t.i + 1)
                nc.vector.tensor_reduce(peak[:, :], by_head(logits[:, s, :]), AX.X, ALU.max).then_inc(l_step, 1)
                dve.wait_ge(l_step, t.i + 1)
                nc.vector.tensor_tensor(by_head(logits[:, s, :]), by_head(logits[:, s, :]), wide(peak[:, :]),
                                        ALU.subtract).then_inc(l_ready, 1)

            def normalise(t):
                s, done = t.slot(2), t.i * WAYS
                dve.wait_ge(exp_done, t.i + 1)
                nc.vector.tensor_reduce(total[:, 0, :], by_head(weights[:, s, :]), AX.X, ALU.add).then_inc(w_step, 1)
                dve.wait_ge(w_step, done + 1)
                nc.vector.reciprocal(total[:, 1, :], total[:, 0, :]).then_inc(w_step, 1)
                dve.wait_ge(w_step, done + 2)
                nc.vector.tensor_tensor(by_head(weights[:, s, :]), by_head(weights[:, s, :]), wide(total[:, 1, :]),
                                        ALU.mult).then_inc(w_ready, 1)

            def step(it):
                for back, stage in ((0, onehots), (1, add_mean), (3, less_peak), (4, normalise), (1, norm)):
                    if it.back(back).exists():
                        stage(it.back(back))
            sweep(dve, 0, LOOP, LOOP_END, END, 4, step)
            dve.wait_ge(tokens_done, TN)
            for c in range(2):
                nc.vector.tensor_copy(token_sum[:, c, :], ps_tok[c][:, :]).then_inc(sums_kept, 1)
            nc.vector.tensor_copy(norm_sum[:, :], ps_norm[:, :]).then_inc(sums_kept, 1)

        @block.tensor
        def _(pe):
            pe.wait_ge(consts_made, 2)
            pe.nop(nofuse=True).then_inc(used, AHEAD)

            def sum_messages(t):
                steps, before = planned(pe, t, 1, TE), planned(pe, t, 2, STEPS_MAX)
                acc = ps_sum[t.slot(2)]
                wait(pe, mean_added, t.i - 1)
                nc.tensor.matmul(acc[:, 0:D + 1], zeros[:, 0:P], zeros[:, :], start=True, stop=False, skip_group_check=True)
                with pe.Fori(0, steps) as i:
                    s = pe.snap(before + i)
                    pe.wait_ge(onehot_ready, s + 1)
                    pe.wait_ge(messages_in, s + 1)
                    hot = onehot[:, bass.ds(pe.snap(s % AHEAD), 1), :].rearrange("p o n -> p (o n)")
                    slot = bass.ds(pe.snap(s % RING), 1)
                    for part in range(3):
                        width = D + (part == 2)
                        done = nc.tensor.matmul(
                            acc[:, 0:width], hot,
                            gathered[:, slot, part * D:part * D + width].rearrange("p o n -> p (o n)"),
                            start=False, stop=False, skip_group_check=True)
                    done.then_inc(used, 1)
                nc.tensor.matmul(acc[:, 0:D + 1], zeros[:, 0:P], zeros[:, :], start=False, stop=True,
                                 skip_group_check=True).then_inc(summed, 1)

            def turn_x(t):
                pe.wait_ge(xn_ready, t.i + 1)
                wait(pe, xt_kept, t.i)
                for c in range(2):
                    done = nc.tensor.transpose(ps_x[:, c * P:(c + 1) * P], xn[:, t.slot(4), c * P:(c + 1) * P], ident[:, :])
                done.then_inc(xt_done, 1)

            def slice_logits(t):
                s = t.slot(2)
                pe.wait_ge(xt_kept, t.i + 1)
                wait(pe, l_kept, t.i)
                nc.tensor.matmul(ps_l[:, :], xn_t[:, s, 0, :], w_logit[:, 0, :], start=True, stop=False)
                nc.tensor.matmul(ps_l[:, :], xn_t[:, s, 1, :], w_logit[:, 1, :], start=False, stop=True).then_inc(l_done, 1)

            def tokens(t):
                s, x4 = t.slot(2), t.slot(4)
                rows = LAST if t.is_last() else P
                pe.wait_ge(w_ready, t.i + 1)
                wait(pe, turned_kept, t.i)
                for c in range(2):
                    nc.tensor.matmul(ps_tok[c][:, :], xn[0:rows, x4, c * P:(c + 1) * P], weights[0:rows, s, :],
                                     start=t.is_first(), stop=t.is_last(), skip_group_check=True)
                nc.tensor.matmul(ps_norm[:, :], ones[0:rows, :], weights[0:rows, s, :], start=t.is_first(),
                                 stop=t.is_last(), skip_group_check=True)
                for c in range(4):
                    done = nc.tensor.transpose(ps_s[:, c * P:(c + 1) * P], weights[:, s, c * P:(c + 1) * P], ident[:, :])
                done.then_inc(tokens_done, 1)

            def step(it):
                for back, stage in ((0, sum_messages), (1, turn_x), (2, slice_logits), (4, tokens)):
                    if it.back(back).exists():
                        stage(it.back(back))
            sweep(pe, 0, LOOP, LOOP_END, END, 4, step)
            steps = planned(pe, TN, 2, STEPS_MAX)
            pe.wait_ge(used, steps + AHEAD)
            pe.nop(nofuse=True).then_inc(used, RING)
            pe.wait_ge(messages_in, planned(pe, TN, 3, STEPS_MAX) * AHEAD + (AHEAD - RING))
            pe.nop(nofuse=True).then_inc(used, AHEAD - RING)

    with ExitStack() as three:
        sb, pb, sem = keeper(three)
        wfx = sb("wfx", [P, 2, HG], f32)
        bfx = sb("bfx", [1, HG], f32)
        wqkv = sb("wqkv", [DH, 3, DH], f32)
        wo = sb("wo", [DH, H, D], f32)
        bo = sb("bo", [P, D], f32)
        rnorm = sb("rnorm", [DH, HG], f32)
        token = sb("token", [DH, HG], f32)
        q_t, k_t, v = sb("q_t", [DH, HG], f32), sb("k_t", [DH, HG], f32), sb("v", [G, HG], f32)
        att, att_t, o_t = sb("att", [G, HG], f32), sb("att_t", [G, HG], f32), sb("o_t", [DH, HG], f32)
        peak3, total3 = sb("peak3", [G, H], f32), sb("total3", [G, 2, H], f32)
        w_final = sb("w_final", [P, 4, D], f32)
        turned = sb("turned3", [P, 4, HG], f32)
        result = sb("result", [P, 4, D], f32)
        ps = [pb(f"ps3_{n}") for n in range(8)]
        weights_in, dve_step, pe_step, act_step = sem("weights_in3"), sem("dve_step"), sem("pe_step"), sem("act_step")
        biased, product, added = sem("biased"), sem("product"), sem("added")
        turned_in = [sem(f"turned_in{j}") for j in range(4)]
        out_done = [sem(f"out_done{j}") for j in range(4)]
        LOOPS = TN // 4 * 4
        block = three.enter_context(nc.Block())

        @block.sync
        def _(sp):
            sp.dma_start(wfx[:, :, :], w_fx.rearrange("(c p) n -> p c n", p=P)).then_inc(weights_in, 16)
            sp.dma_start(bfx[:, :], b_fx.rearrange("(o n) -> o n", o=1)).then_inc(weights_in, 16)
            for j, w in enumerate((w_q, w_k, w_v)):
                sp.dma_start(wqkv[:, j, :], w).then_inc(weights_in, 16)
            sp.dma_start(wo[:, :, :], w_out.rearrange("(h d) n -> d h n", d=DH)).then_inc(weights_in, 16)
            sp.dma_start(bo[:, :], b_out.rearrange("(o n) -> o n", o=1).broadcast_to([P, D])).then_inc(weights_in, 16)

            def load(t):
                s = t.slot(4)
                wait(sp, product, t.i - 3)
                sp.dma_start(turned[:, s, :],
                             weights_t[bass.ds(t.i, 1), :, :].rearrange("o p n -> p (o n)")).then_inc(turned_in[s], 16)
            sweep(sp, 0, 4, LOOPS, TN - 1, 4, load)

        @block.gpsimd
        def _(pool):
            pool.wait_ge(weights_in, 112)

            def bias(t):
                nc.gpsimd.tensor_tensor(x_tile(t), x_tile(t), bo[:, :], ALU.add).then_inc(biased, 1)
            sweep(pool, 0, 0, LOOPS, TN - 1, 4, bias)

        @block.scalar
        def _(act):
            nc.scalar.preload_act_table(ACT.Exp)
            act.wait_ge(pe_step, 2)
            nc.scalar.copy(k_t[:, :], ps[2][0:DH, :]).then_inc(act_step, 1)
            act.wait_ge(dve_step, 7)
            nc.scalar.activation(att[:, :], att[:, :], ACT.Exp, scale=float(DH) ** -0.5).then_inc(act_step, 1)

            def store(t):
                s = t.slot(4)
                act.wait_ge(added, t.i + 1)
                if t.is_last():
                    act.dma_start(out[(TN - 1) * P:N, :], result[0:LAST, s, :]).then_inc(out_done[s], 16)
                else:
                    act.dma_start(out[bass.ds(t.i * P, P), :], result[:, s, :]).then_inc(out_done[s], 16)
            sweep(act, 0, 0, LOOPS, TN - 1, 4, store)
            for s in range(4):
                act.wait_ge(out_done[s], 16 * ((TN - s + 3) // 4))

        @block.vector
        def _(dve):
            def by_head(a):
                return a[:, :].rearrange("p (h g) -> p h g", h=H)

            def wide(a):
                return a.rearrange("p (h o) -> p h o", o=1).broadcast_to([a.shape[0], H, G])
            nc.vector.tensor_scalar(rnorm[:, :], norm_sum[0:DH, :], 1e-5, None, ALU.add).then_inc(dve_step, 1)
            dve.wait_ge(dve_step, 1)
            nc.vector.reciprocal(rnorm[:, :], rnorm[:, :]).then_inc(dve_step, 1)
            dve.wait_ge(dve_step, 2)
            dve.wait_ge(pe_step, 1)
            nc.vector.tensor_tensor(token[:, :], ps[0][0:DH, :], rnorm[:, :], ALU.mult).then_inc(dve_step, 1)
            dve.wait_ge(pe_step, 2)
            nc.vector.tensor_copy(q_t[:, :], ps[1][0:DH, :]).then_inc(dve_step, 1)
            dve.wait_ge(pe_step, 3)
            nc.vector.tensor_copy(v[:, :], ps[3][0:G, :]).then_inc(dve_step, 1)
            dve.wait_ge(pe_step, 4)
            nc.vector.tensor_reduce(peak3[:, :], ps[4][0:G, :].rearrange("p (h g) -> p h g", h=H), AX.X, ALU.max).then_inc(dve_step, 1)
            dve.wait_ge(dve_step, 6)
            nc.vector.tensor_tensor(by_head(att), ps[4][0:G, :].rearrange("p (h g) -> p h g", h=H), wide(peak3[:, :]),
                                    ALU.subtract).then_inc(dve_step, 1)
            dve.wait_ge(act_step, 2)
            nc.vector.tensor_reduce(total3[:, 0, :], by_head(att), AX.X, ALU.add).then_inc(dve_step, 1)
            dve.wait_ge(dve_step, 8)
            nc.vector.reciprocal(total3[:, 1, :], total3[:, 0, :]).then_inc(dve_step, 1)
            dve.wait_ge(dve_step, 9)
            nc.vector.tensor_tensor(by_head(att), by_head(att), wide(total3[:, 1, :]), ALU.mult).then_inc(dve_step, 1)
            dve.wait_ge(pe_step, 5)
            nc.vector.tensor_copy(att_t[:, :], ps[5][0:G, :]).then_inc(dve_step, 1)
            dve.wait_ge(pe_step, 6)
            nc.vector.tensor_copy(o_t[:, :], ps[0][0:DH, :]).then_inc(dve_step, 1)
            dve.wait_ge(pe_step, 7)
            for n in range(2):
                nc.vector.tensor_copy(w_final[:, 2 * n:2 * n + 2, :],
                                      ps[6 + n][:, :].rearrange("p (c d) -> p c d", c=2)).then_inc(dve_step, 1)

            def add(t):
                s = t.slot(4)
                dve.wait_ge(biased, t.i + 1)
                wait(dve, out_done[s], t.round(4) * 16)
                dve.wait_ge(product, t.i + 1)
                nc.vector.tensor_tensor(result[:, s, :], ps[s][:, 0:D], x_tile(t), ALU.add).then_inc(added, 1)
            sweep(dve, 0, 4, LOOPS, TN - 1, 4, add)

        @block.tensor
        def _(pe):
            def head(h):
                return slice(h * G, (h + 1) * G)
            pe.wait_ge(weights_in, 112)
            for h in range(H):
                for c in range(2):
                    nc.tensor.matmul(ps[0][0:DH, head(h)], wfx[:, c, head(h)], token_sum[:, c, head(h)], start=(c == 0), stop=False)
                done = nc.tensor.matmul(ps[0][0:DH, head(h)], bfx[0:1, head(h)], norm_sum[0:1, head(h)], start=False, stop=True)
            done.then_inc(pe_step, 1)
            pe.wait_ge(dve_step, 3)
            nc.tensor.matmul(ps[1][0:DH, :], wqkv[:, 0, :], token[:, :], start=True, stop=True)
            nc.tensor.matmul(ps[2][0:DH, :], wqkv[:, 1, :], token[:, :], start=True, stop=True).then_inc(pe_step, 1)
            for h in range(H):
                done = nc.tensor.matmul(ps[3][0:G, head(h)], token[:, head(h)], wqkv[:, 2, :], start=True, stop=True)
            done.then_inc(pe_step, 1)
            pe.wait_ge(dve_step, 4)
            pe.wait_ge(act_step, 1)
            for h in range(H):
                done = nc.tensor.matmul(ps[4][0:G, head(h)], q_t[:, head(h)], k_t[:, head(h)], start=True, stop=True)
            done.then_inc(pe_step, 1)
            pe.wait_ge(dve_step, 10)
            for h in range(H):
                done = nc.tensor.transpose(ps[5][0:G, head(h)], att[:, head(h)], ident[0:G, 0:G])
            done.then_inc(pe_step, 1)
            pe.wait_ge(dve_step, 11)
            for h in range(H):
                done = nc.tensor.matmul(ps[0][0:DH, head(h)], v[:, head(h)], att_t[:, head(h)], start=True, stop=True)
            done.then_inc(pe_step, 1)
            pe.wait_ge(dve_step, 12)
            for h in range(H):
                c, r = h // 2, h % 2 * G
                done = nc.tensor.matmul(ps[6 + c // 2][r:r + G, c % 2 * D:(c % 2 + 1) * D], o_t[:, head(h)], wo[:, h, :],
                                        start=True, stop=True)
            done.then_inc(pe_step, 1)
            pe.wait_ge(dve_step, 14)

            def multiply(t):
                s = t.slot(4)
                pe.wait_ge(turned_in[s], t.round(4) * 16 + 16)
                wait(pe, added, t.i - 3)
                for c in range(4):
                    done = nc.tensor.matmul(ps[s][:, 0:D], turned[:, s, c * P:(c + 1) * P], w_final[:, c, :],
                                            start=(c == 0), stop=(c == 3))
                done.then_inc(product, 1)
            sweep(pe, 0, 4, LOOPS, TN - 1, 4, multiply)

    whole.close()


INPUTS = ['x', 'src', 'dst', 'L0_gnn_W_self', 'L0_gnn_W_neigh', 'L0_ffn_W_fx', 'L0_ffn_b_fx', 'L0_ffn_W_x',
          'L0_ffn_b_x', 'L0_ffn_W_slice', 'L0_ffn_b_slice', 'L0_ffn_W_q', 'L0_ffn_W_k', 'L0_ffn_W_v',
          'L0_ffn_W_out', 'L0_ffn_b_out', 'L0_ffn_temperature']


def kernel(**inputs):
    import concourse.bacc as bacc
    from concourse.bass_utils import run_bass_kernel_spmd

    nc = bacc.Bacc("TRN2", target_bir_lowering=False, num_devices=1)
    arrays, args = {}, []
    for name in INPUTS:
        a = np.ascontiguousarray(inputs[name])
        arrays[f"in_{name}"] = a
        args.append(nc.dram_tensor(f"in_{name}", a.shape, mybir.dt.from_np(a.dtype), kind="ExternalInput").ap())
    out = nc.dram_tensor("out", (N, D), mybir.dt.float32, kind="ExternalOutput").ap()
    build(nc, *args, out)
    return run_bass_kernel_spmd(nc, [arrays], core_ids=[0]).results[0]["out"]
```

```python
from contextlib import ExitStack

import concourse.bass as bass
import numpy as np
from concourse import mybir

P = 128
N = 12500
D = 256
E = 200000
TOPK = 32
H = 8
DH = 64
G = 64
HG = H * G
TN = -(-N // P)
LAST = N - (TN - 1) * P
TE = -(-E // P)
CH = -(-TE // P)
FULL_E = E // P
LEFT_E = E - FULL_E * P
FULL_CH = FULL_E // P
LEFT_CH = FULL_E - FULL_CH * P
TU = TN // 2
RING = 8
AHEAD = 16
EPS = 1e-5
TAKEN = -3.0e38
FAR = float(1 << 20)
MAXE = 4096.0
XCH = 14


class Tile:

    def __init__(self, k, step, at, count):
        self.k, self.step, self.at, self.count = k, step, at, count
        self.i = at if isinstance(k, int) else k * step + at

    def back(self, d):
        return Tile(self.k, self.step, self.at - d, self.count)

    def half(self, a):
        return Tile(self.k, self.step * 2, self.at * 2 + a, self.count * 2)

    def exists(self):
        return not isinstance(self.k, int) or 0 <= self.at < self.count

    def is_first(self):
        return isinstance(self.k, int) and self.at == 0

    def is_last(self):
        return isinstance(self.k, int) and self.at == self.count - 1

    def slot(self, m):
        return self.at % m

    def round(self, m):
        return self.at // m if isinstance(self.k, int) else self.k * (self.step // m) + self.at // m


def sweep(eng, first, loop_from, loop_to, last, unroll, body, count=TN):
    for t in range(first, loop_from):
        body(Tile(0, 0, t, count))
    with eng.Fori(0, (loop_to - loop_from) // unroll) as k:
        for u in range(unroll):
            body(Tile(k, unroll, loop_from + u, count))
    for t in range(loop_to, last + 1):
        body(Tile(0, 0, t, count))


def wait(eng, sem, count):
    if not (isinstance(count, int) and count <= 0):
        eng.wait_ge(sem, count)


def build(nc, x, src, dst, w_self, w_neigh, w_fx, b_fx, w_x, b_x, w_slice, b_slice, w_q, w_k, w_v, w_out, b_out,
          temperature, out):
    f32, bf16, i32 = mybir.dt.float32, mybir.dt.bfloat16, mybir.dt.int32
    ALU, ACT, AX = mybir.AluOpType, mybir.ActivationFunctionType, mybir.AxisListType

    messages = nc.dram_tensor("messages", [TN * P, 3 * D], bf16, kind="Internal").ap()
    weights_t = nc.dram_tensor("weights_t", [TN, P, HG], f32, kind="Internal").ap()
    plan_dram = nc.dram_tensor("plan_dram", [TN + 1, 4], i32, kind="Internal").ap()

    whole = ExitStack()

    def keeper(stack):
        return (lambda name, shape, dt: stack.enter_context(nc.sbuf_tensor(name, shape, dt)),
                lambda name: stack.enter_context(nc.psum_tensor(name, [P, 512], f32)),
                lambda name: stack.enter_context(nc.semaphore(name)))

    sb, _, _ = keeper(whole)
    x_all = sb("x_all", [P, TN, D], f32)
    src_cols = sb("src_cols", [P, CH * P], f32)
    dst_cols = sb("dst_cols", [P, CH * P], f32)
    plan = sb("plan", [1, (TN + 1) * 4], i32)
    window = sb("window", [P, TN + 1], f32)
    node_row = sb("node_row", [P, P], f32)
    ident = sb("ident", [P, P], f32)
    ones = sb("ones", [P, P], f32)
    w_logit = sb("w_logit", [P, 2, HG], f32)
    b_logit = sb("b_logit", [P, HG], f32)
    token_sum = sb("token_sum", [P, 2, HG], f32)
    norm_sum = sb("norm_sum", [P, HG], f32)

    def x_tile(t):
        return x_all[:, bass.ds(t.i, 1), :].rearrange("p o d -> p (o d)")

    with ExitStack() as one:
        sb, pb, sem = keeper(one)
        src_int = sb("src_int", [P, CH, P], i32)
        dst_int = sb("dst_int", [P, CH, P], i32)
        src_f = src_int[:, :, :].bitcast(f32)
        dst_f = dst_int[:, :, :].bitcast(f32)
        tail_f = sb("tail_f", [P, P], f32)
        node_int = sb("node_int", [P, P], i32)
        win_int = sb("win_int", [P, TN + 1], i32)
        edge_int = sb("edge_int", [P, CH], i32)
        edge_no = sb("edge_no", [P, CH], f32)
        dmin = sb("dmin", [P, CH], f32)
        dmax = sb("dmax", [P, CH], f32)
        starts = sb("starts", [P, TN, CH], f32)
        needed = sb("needed", [P, TN, CH], f32)
        last_part = sb("last_part", [P, TN], f32)
        first_part = sb("first_part", [P, TN], f32)
        earlier = sb("earlier", [P, P], f32)
        plan_f = sb("plan_f", [P, 4], f32)
        cols = sb("cols", [P, 8], f32)
        pairs_int = sb("pairs_int", [P, 1], i32)
        plan_i = sb("plan_i", [P, 4], i32)
        w_both = sb("w_both", [P, 2, 2 * D], f32)
        wx = sb("wx", [P, 2, HG], f32)
        wx_t = sb("wx_t", [P, 4, D], f32)
        ws_pair = sb("ws_pair", [P, P], f32)
        bx_cols = sb("bx_cols", [P, 4], f32)
        bx_wide = sb("bx_wide", [P, 4, P], f32)
        bs_row = sb("bs_row", [P, G], f32)
        temp = sb("temp", [P, H], f32)
        rtemp = sb("rtemp", [P, H], f32)
        eps = sb("eps", [P, 1], f32)
        stats = sb("stats", [P, 2, 2, 6], f32)
        mv = sb("mv", [P, 2, 2, 2], f32)
        std = sb("std", [P, 2, 2], f32)
        rstd = sb("rstd", [P, 2, 2], f32)
        shift = sb("shift", [P, 2, 2], f32)
        xn = sb("xn", [P, 2, 2, D], f32)
        xn_t = sb("xn_t", [P, 2, 4 * P], f32)
        neigh = sb("neigh", [P, 4, 2, D], f32)
        left = sb("left", [P, 2, 2, D], f32)
        top8 = sb("top8", [P, 2, 4, 8], f32)
        mask = sb("mask", [P, 2, D], f32)
        sparse = sb("sparse", [P, 2, 2, D], f32)
        rest = sb("rest", [P, 2, 2, D], f32)
        parts = sb("parts", [P, 2, 2, 3 * D], bf16)
        ps_t = [pb("ps_t0"), pb("ps_t1")]
        ps_h = [one.enter_context(nc.psum_tensor(f"ps_h{n}", [P, 2, 512], f32)) for n in range(2)]
        ps_p = [pb("ps_p0"), pb("ps_p1")]
        ps_w = [ps_h[1][:, 0, :], ps_h[1][:, 1, :]]

        pads_set, edges_in, weights_in, x_in = sem("pads_set"), sem("edges_in"), sem("weights_in"), sem("x_in")
        tables_made, consts_made, prep, prep_pe, prep_act = (
            sem("tables_made"), sem("consts_made"), sem("prep"), sem("prep_pe"), sem("prep_act"))
        plan_out, plan_in = sem("plan_out"), sem("plan_in")
        stats_made, means_made, std_made, rstd_made, shift_made, centred = (
            sem("stats_made"), sem("means_made"), sem("std_made"), sem("rstd_made"), sem("shift_made"),
            sem("centred"))
        xn_done, xt_done, xt_kept, h_done, neigh_kept, base_kept, mask_done, sparse_done = (
            sem("xn_done"), sem("xt_done"), sem("xt_kept"), sem("h_done"), sem("neigh_kept"),
            sem("base_kept"), sem("mask_done"), sem("sparse_done"))
        top_step = [sem("top_step0"), sem("top_step1")]
        part1, rest1, part2, part3 = sem("part1"), sem("rest1"), sem("part2"), sem("part3")
        stored = [sem("stored0"), sem("stored1")]
        FIRST, LOOP, LOOP_END, END = -3, 3, TU - 6, TU
        TOPS = 8
        block = one.enter_context(nc.Block())

        @block.sync
        def _(sp):
            sp.wait_ge(pads_set, 3)
            for rows, ints in ((dst, dst_int), (src, src_int)):
                sp.dma_start(ints[:, 0:FULL_CH, :],
                             rows[0:FULL_CH * P * P].rearrange("(c p n) -> p c n", p=P, n=P)).then_inc(edges_in, 16)
                sp.dma_start(ints[0:LEFT_CH, FULL_CH, :],
                             rows[FULL_CH * P * P:FULL_E * P].rearrange("(p n) -> p n", n=P)).then_inc(edges_in, 16)
                sp.dma_start(ints[LEFT_CH:LEFT_CH + 1, FULL_CH, 0:LEFT_E],
                             rows[FULL_E * P:E].rearrange("(p n) -> p n", p=1)).then_inc(edges_in, 16)
            sp.dma_start(wx[:, :, :], w_x.rearrange("(c p) n -> p c n", p=P)).then_inc(weights_in, 16)
            sp.dma_start(ws_pair[0:G, 0:G], w_slice).then_inc(weights_in, 16)
            sp.dma_start(ws_pair[G:P, G:P], w_slice).then_inc(weights_in, 16)
            with nc.allow_non_contiguous_dma(reason="512 single values, once"):
                sp.dma_start(bx_cols[:, :], b_x.rearrange("(c p) -> p c", p=P)).then_inc(weights_in, 16)
            sp.dma_start(bs_row[:, :], b_slice.rearrange("(o n) -> o n", o=1).broadcast_to([P, G])).then_inc(weights_in, 16)
            sp.dma_start(temp[:, :], temperature.rearrange("a h b c -> a (h b c)").broadcast_to([P, H])).then_inc(weights_in, 16)
            sp.dma_start(w_both[:, :, 0:D], w_self.rearrange("(c p) n -> p c n", p=P)).then_inc(weights_in, 16)
            sp.dma_start(w_both[:, :, D:2 * D], w_neigh.rearrange("(c p) n -> p c n", p=P)).then_inc(weights_in, 16)
            for a in range(0, TN - 1, XCH):
                b = min(a + XCH, TN - 1)
                sp.dma_start(x_all[:, a:b, :], x[a * P:b * P, :].rearrange("(t p) d -> p t d", p=P)).then_inc(x_in, 16)
            sp.dma_start(x_all[0:LAST, TN - 1, :], x[(TN - 1) * P:N, :]).then_inc(x_in, 16)
            sp.wait_ge(prep, 27)
            sp.dma_start(plan_dram, plan_i[0:TN + 1, :]).then_inc(plan_out, 16)
            sp.wait_ge(plan_out, 16)
            sp.dma_start(plan[:, :], plan_dram.rearrange("t f -> (t f)").rearrange("(o n) -> o n", o=1)).then_inc(plan_in, 16)

            def store(u):
                sp.wait_ge(part3, u.i + 1)
                sp.dma_start(messages[bass.ds(u.i * (2 * P), 2 * P), :].rearrange("(a p) n -> p a n", a=2),
                             parts[:, u.slot(2), :, :]).then_inc(stored[u.slot(2)], 16)
            sweep(sp, 0, 0, TU - 1, TU - 1, 2, store, TU)
            sp.wait_ge(plan_in, 16)
            for n, s in enumerate(stored):
                sp.wait_ge(s, 16 * ((TU + 1 - n) // 2))

        @block.gpsimd
        def _(pool):
            nc.gpsimd.iota(win_int[:, :], pattern=[[P, TN + 1]], base=0, channel_multiplier=0).then_inc(tables_made, 1)
            nc.gpsimd.iota(edge_int[:, :], pattern=[[P, CH]], base=1, channel_multiplier=1).then_inc(tables_made, 1)
            nc.gpsimd.iota(node_int[:, :], pattern=[[1, P]], base=0, channel_multiplier=0).then_inc(tables_made, 1)
            pool.wait_ge(consts_made, 3)
            nc.gpsimd.affine_select(out=ident[:, :], in_=ident[:, :], compare_op=ALU.not_equal, fill=1.0, base=0,
                                    pattern=[[-1, P]], channel_multiplier=1).then_inc(tables_made, 1)
            nc.gpsimd.affine_select(out=earlier[:, :], in_=earlier[:, :], compare_op=ALU.is_ge, fill=1.0, base=0,
                                    pattern=[[-1, P]], channel_multiplier=1).then_inc(tables_made, 1)

            def split(it):
                u = it.back(1)
                if not u.exists():
                    return
                s = u.slot(2)
                pool.wait_ge(top_step[0], u.i * TOPS + TOPS)
                pool.wait_ge(top_step[1], u.i * TOPS + TOPS)
                wait(pool, sparse_done, u.i)
                pool.nop(nofuse=True)
                nc.gpsimd.tensor_scalar(mask[:, :, :], left[:, s, :, :], TAKEN, None, ALU.is_equal).then_inc(mask_done, 1)
                pool.wait_ge(mask_done, u.i + 1)
                nc.gpsimd.tensor_tensor(sparse[:, s, :, :], mask[:, :, :], neigh[:, u.slot(4), :, :], ALU.mult).then_inc(sparse_done, 1)
                pool.wait_ge(part1, u.i + 1)
                nc.gpsimd.tensor_tensor(rest[:, s, :, :], sparse[:, s, :, :], parts[:, s, :, 0:D], ALU.subtract).then_inc(rest1, 1)
                pool.wait_ge(part2, u.i + 1)
                nc.gpsimd.tensor_tensor(parts[:, s, :, 2 * D:3 * D], rest[:, s, :, :], parts[:, s, :, D:2 * D],
                                        ALU.subtract).then_inc(part3, 1)
            sweep(pool, FIRST, LOOP, LOOP_END, END, 4, split, TU)

        @block.scalar
        def _(act):
            nc.scalar.preload_act_table(ACT.Sqrt)
            for n in range(8):
                full = n % 4 < 3
                cols_of = src_cols if n < 4 else dst_cols
                width = 4 * P if full else (CH - 12) * P
                act.wait_ge(prep_pe, n + 1)
                nc.scalar.copy(cols_of[:, (n % 4) * 4 * P:(n % 4) * 4 * P + width],
                               ps_t[n % 2][:, 0:width]).then_inc(prep_act, 1)
            act.wait_ge(prep_pe, 9)
            nc.scalar.copy(wx_t[:, 0:2, :], ps_w[0].rearrange("p (a k) -> p a k", a=2)).then_inc(prep_act, 1)
            act.wait_ge(prep_pe, 10)
            nc.scalar.copy(wx_t[:, 2:4, :], ps_w[1].rearrange("p (a k) -> p a k", a=2)).then_inc(prep_act, 1)

            act.wait_ge(consts_made, 4)

            def step(it):
                u = it.back(-3)
                if u.exists():
                    s = u.slot(2)
                    act.wait_ge(means_made, u.i + 1)
                    wait(act, rstd_made, u.i - 1)
                    nc.scalar.activation(std[:, s, :], mv[:, s, :, 1], ACT.Sqrt, bias=eps[:, :]).then_inc(std_made, 1)
                u = it.back(-2)
                if u.exists():
                    s = u.slot(2)
                    act.wait_ge(rstd_made, u.i + 1)
                    act.wait_ge(shift_made, u.i + 1)
                    wait(act, xt_done, u.i - 1)
                    for a in range(2):
                        nc.scalar.activation(xn[:, s, a, :], x_tile(u.half(a)), ACT.Identity,
                                             bias=shift[:, s, a:a + 1]).then_inc(centred, 1)
                    act.wait_ge(centred, u.i * 2 + 2)
                    for a in range(2):
                        done = nc.scalar.activation(xn[:, s, a, :], xn[:, s, a, :], ACT.Identity,
                                                    scale=rstd[:, s, a:a + 1])
                    done.then_inc(xn_done, 1)
                u = it.back(-1)
                if u.exists():
                    s = u.slot(2)
                    act.wait_ge(h_done, u.i + 1)
                    wait(act, sparse_done, u.i - 3)
                    nc.scalar.copy(neigh[:, u.slot(4), :, :], ps_h[s][:, :, D:2 * D]).then_inc(neigh_kept, 1)
                    nc.scalar.copy(x_all[:, bass.ds(u.i * 2, 2), :], ps_h[s][:, :, 0:D]).then_inc(base_kept, 1)
                u = it.back(1)
                if u.exists():
                    s = u.slot(2)
                    act.wait_ge(sparse_done, u.i + 1)
                    wait(act, stored[s], u.round(2) * 16)
                    nc.scalar.copy(parts[:, s, :, 0:D], sparse[:, s, :, :]).then_inc(part1, 1)
                u = it.back(-2)
                if u.exists():
                    s = u.slot(2)
                    act.wait_ge(xt_done, u.i + 1)
                    wait(act, h_done, u.i - 1)
                    nc.scalar.copy(xn_t[:, s, :], ps_t[s][:, :]).then_inc(xt_kept, 1)
                u = it.back(1)
                if u.exists():
                    s = u.slot(2)
                    act.wait_ge(rest1, u.i + 1)
                    nc.scalar.copy(parts[:, s, :, D:2 * D], rest[:, s, :, :]).then_inc(part2, 1)
            sweep(act, FIRST, LOOP, LOOP_END, END, 4, step, TU)

        @block.vector
        def _(dve):
            nc.vector.memset(dst_int[:, FULL_CH, :], -1).then_inc(pads_set, 1)
            nc.vector.memset(src_int[:, FULL_CH, :], 0).then_inc(pads_set, 1)
            nc.vector.memset(x_all[:, TN - 1, :], 0.0)
            nc.vector.memset(ws_pair[:, :], 0.0).then_inc(pads_set, 1)
            nc.vector.memset(ident[:, :], 0.0).then_inc(consts_made, 1)
            nc.vector.memset(earlier[:, :], 0.0).then_inc(consts_made, 1)
            nc.vector.memset(ones[:, :], 1.0).then_inc(consts_made, 1)
            nc.vector.memset(eps[:, :], EPS).then_inc(consts_made, 1)
            nc.vector.memset(plan_f[:, :], 1.0)
            dve.wait_ge(tables_made, 3)
            nc.vector.tensor_copy(window[:, :], win_int[:, :])
            nc.vector.tensor_copy(edge_no[:, :], edge_int[:, :])
            nc.vector.tensor_copy(node_row[:, :], node_int[:, :])
            dve.wait_ge(edges_in, 96)
            nc.vector.tensor_copy(src_f, src_int[:, :, :]).then_inc(prep, 1)
            nc.vector.tensor_copy(dst_f, dst_int[:, :, :]).then_inc(prep, 1)
            dve.wait_ge(prep, 2)
            nc.vector.tensor_reduce(dmax[:, :], dst_f, AX.X, ALU.max).then_inc(prep, 1)
            nc.vector.tensor_reduce(dmin[:, 0:FULL_CH], dst_f[:, 0:FULL_CH, :], AX.X, ALU.min).then_inc(prep, 1)
            nc.vector.tensor_scalar(tail_f[:, :], dst_f[:, FULL_CH, :], 0.0, FAR, ALU.is_lt, ALU.mult).then_inc(prep, 1)
            dve.wait_ge(prep, 5)
            nc.vector.tensor_tensor(tail_f[:, :], tail_f[:, :], dst_f[:, FULL_CH, :], ALU.add).then_inc(prep, 1)
            dve.wait_ge(prep, 6)
            nc.vector.tensor_reduce(dmin[:, FULL_CH:CH], tail_f[:, :], AX.X, ALU.min).then_inc(prep, 1)
            dve.wait_ge(prep, 7)
            shape = [P, TN, CH]

            def per_edge_tile(a):
                return a[:, :].rearrange("p (o c) -> p o c", o=1).broadcast_to(shape)

            def per_node_tile(a, at):
                return a[:, at:at + TN].rearrange("p (t o) -> p t o", o=1).broadcast_to(shape)
            nc.vector.tensor_tensor(starts[:, :, :], per_edge_tile(dmin), per_node_tile(window, 1), ALU.is_lt).then_inc(prep, 1)
            nc.vector.tensor_tensor(needed[:, :, :], per_edge_tile(dmax), per_node_tile(window, 0), ALU.is_ge).then_inc(prep, 1)
            dve.wait_ge(prep, 9)
            nc.vector.tensor_tensor(needed[:, :, :], needed[:, :, :], starts[:, :, :], ALU.mult).then_inc(prep, 1)
            dve.wait_ge(prep, 10)
            nc.vector.tensor_tensor(starts[:, :, :], needed[:, :, :], per_edge_tile(edge_no), ALU.mult).then_inc(prep, 1)
            dve.wait_ge(prep, 11)
            nc.vector.tensor_reduce(last_part[:, :], starts[:, :, :], AX.X, ALU.max).then_inc(prep, 1)
            nc.vector.tensor_scalar(edge_no[:, :], edge_no[:, :], -1.0, MAXE, ALU.mult, ALU.add).then_inc(prep, 1)
            dve.wait_ge(prep, 13)
            nc.vector.tensor_tensor(needed[:, :, :], needed[:, :, :], per_edge_tile(edge_no), ALU.mult).then_inc(prep, 1)
            dve.wait_ge(prep, 14)
            nc.vector.tensor_reduce(first_part[:, :], needed[:, :, :], AX.X, ALU.max).then_inc(prep, 1)
            dve.wait_ge(prep_pe, 11)
            nc.vector.tensor_reduce(cols[0:TN, 0:2], ps_p[0][0:TN, 0:2 * P].rearrange("t (a p) -> t a p", a=2), AX.X,
                                    ALU.max).then_inc(prep, 1)
            dve.wait_ge(prep, 16)
            nc.vector.tensor_scalar(cols[0:TN, 2:3], cols[0:TN, 0:1], 1.0, None, ALU.min).then_inc(prep, 1)
            nc.vector.tensor_scalar(cols[0:TN, 3:4], cols[0:TN, 1:2], -1.0, MAXE - 1.0, ALU.mult, ALU.add).then_inc(prep, 1)
            dve.wait_ge(prep, 18)
            nc.vector.tensor_tensor(plan_f[0:TN, 0:1], cols[0:TN, 2:3], cols[0:TN, 3:4], ALU.mult).then_inc(prep, 1)
            dve.wait_ge(prep, 19)
            nc.vector.tensor_tensor(cols[0:TN, 4:5], cols[0:TN, 0:1], plan_f[0:TN, 0:1], ALU.subtract).then_inc(prep, 1)
            dve.wait_ge(prep, 20)
            nc.vector.tensor_scalar(pairs_int[0:TN, :], cols[0:TN, 4:5], 1.0, 1.0, ALU.max, ALU.add).then_inc(prep, 1)
            dve.wait_ge(prep, 21)
            nc.vector.tensor_scalar(pairs_int[0:TN, :], pairs_int[0:TN, :], 1, None, ALU.arith_shift_right).then_inc(prep, 1)
            dve.wait_ge(prep, 22)
            nc.vector.tensor_copy(plan_f[0:TN, 1:2], pairs_int[0:TN, :]).then_inc(prep, 1)
            dve.wait_ge(prep_pe, 12)
            nc.vector.tensor_copy(plan_f[0:TN + 1, 2:3], ps_p[1][0:TN + 1, 0:1]).then_inc(prep, 1)
            nc.vector.tensor_scalar(plan_f[0:TN + 1, 3:4], ps_p[1][0:TN + 1, 0:1], -1.0, None,
                                    ALU.add).then_inc(prep, 1)
            dve.wait_ge(prep, 25)
            nc.vector.tensor_copy(plan_i[0:TN + 1, :], plan_f[0:TN + 1, :]).then_inc(prep, 1)
            dve.wait_ge(prep, 26)
            nc.vector.tensor_scalar(plan_i[0:TN + 1, 3:4], plan_i[0:TN + 1, 3:4], AHEAD.bit_length() - 1, None,
                                    ALU.arith_shift_right).then_inc(prep, 1)
            dve.wait_ge(weights_in, 128)
            nc.vector.tensor_scalar(temp[:, :], temp[:, :], 0.1, 5.0, ALU.max, ALU.min).then_inc(prep, 1)
            nc.vector.tensor_copy(bx_wide[:, :, :],
                                  bx_cols[:, :].rearrange("p (c o) -> p c o", o=1).broadcast_to([P, 4, P])).then_inc(prep, 1)
            dve.wait_ge(prep, 29)
            nc.vector.reciprocal(rtemp[:, :], temp[:, :]).then_inc(prep, 1)
            dve.wait_ge(prep, 30)
            by_head = rtemp[:, :].rearrange("p (h o) -> p h o", o=1).broadcast_to([P, H, G])
            for c in range(2):
                dve.wait_ge(prep_pe, 13 + c)
                nc.vector.tensor_tensor(w_logit[:, c, :].rearrange("p (h g) -> p h g", h=H),
                                        ps_w[c].rearrange("p (h g) -> p h g", h=H), by_head,
                                        ALU.mult).then_inc(prep, 1)
            dve.wait_ge(prep_pe, 15)
            b_heads = b_logit[:, :].rearrange("p (h g) -> p h g", h=H)
            nc.vector.tensor_tensor(b_heads, ps_p[0][:, :].rearrange("p (h g) -> p h g", h=H),
                                    bs_row[:, :].rearrange("p (o g) -> p o g", o=1).broadcast_to([P, H, G]),
                                    ALU.add).then_inc(prep, 1)
            dve.wait_ge(prep, 33)
            nc.vector.tensor_tensor(b_heads, b_heads, by_head, ALU.mult).then_inc(prep, 1)
            dve.wait_ge(x_in, 16 * (-(-(TN - 1) // XCH) + 1))

            def means(u):
                s = u.slot(2)
                for a in range(2):
                    done = nc.vector.bn_stats(stats[:, s, a, :], x_tile(u.half(a)))
                done.then_inc(stats_made, 1)
                dve.wait_ge(stats_made, u.i + 1)
                wait(dve, std_made, u.i - 1)
                dve.nop(nofuse=True)
                for a in range(2):
                    done = nc.vector.bn_aggr(mv[:, s, a, :], stats[:, s, a, :])
                done.then_inc(means_made, 1)

            def shifts(u):
                s = u.slot(2)
                dve.wait_ge(std_made, u.i + 1)
                wait(dve, xn_done, u.i - 1)
                nc.vector.reciprocal(rstd[:, s, :], std[:, s, :]).then_inc(rstd_made, 1)
                nc.vector.tensor_scalar(shift[:, s, :], mv[:, s, :, 0], -1.0, None, ALU.mult).then_inc(shift_made, 1)

            def top(u):
                s, done = u.slot(2), dve.snap(u.i * TOPS) if not isinstance(u.i, int) else u.i * TOPS
                dve.wait_ge(neigh_kept, u.i + 1)
                wait(dve, mask_done, u.i - 1)
                dve.nop(nofuse=True)
                for r in range(TOPK // 8):
                    for a in range(2):
                        seen = neigh[:, u.slot(4), a, :] if r == 0 else left[:, s, a, :]
                        if r > 0:
                            dve.wait_ge(top_step[a], done + 2 * r)
                            dve.nop(nofuse=True)
                        nc.vector.max(top8[:, a, r, :], seen).then_inc(top_step[a], 1)
                    for a in range(2):
                        seen = neigh[:, u.slot(4), a, :] if r == 0 else left[:, s, a, :]
                        dve.wait_ge(top_step[a], done + 2 * r + 1)
                        dve.nop(nofuse=True)
                        nc.vector.match_replace(left[:, s, a, :], top8[:, a, r, :], seen, TAKEN).then_inc(top_step[a], 1)

            def step(it):
                if it.back(-3).exists():
                    means(it.back(-3))
                if it.back(-2).exists():
                    shifts(it.back(-2))
                if it.exists():
                    top(it)
            sweep(dve, FIRST, LOOP, LOOP_END, END, 4, step, TU)

        @block.tensor
        def _(pe):
            pe.wait_ge(tables_made, 5)
            pe.wait_ge(prep, 2)
            for n in range(8):
                rows = src_f if n < 4 else dst_f
                chunks = range((n % 4) * 4, min((n % 4) * 4 + 4, CH))
                wait(pe, prep_act, n - 1)
                for c in chunks:
                    done = nc.tensor.transpose(ps_t[n % 2][:, (c % 4) * P:(c % 4 + 1) * P], rows[:, c, :], ident[:, :])
                done.then_inc(prep_pe, 1)
            pe.wait_ge(weights_in, 128)
            for n in range(2):
                for c in range(2):
                    for k in range(2):
                        at = (2 * c + k) * P
                        done = nc.tensor.transpose(ps_w[n][:, at:at + P], wx[:, k, (2 * n + c) * P:(2 * n + c + 1) * P],
                                                   ident[:, :])
                done.then_inc(prep_pe, 1)
            pe.wait_ge(prep, 15)
            nc.tensor.transpose(ps_p[0][0:TN, 0:P], last_part[:, :], ident[:, :])
            nc.tensor.transpose(ps_p[0][0:TN, P:2 * P], first_part[:, :], ident[:, :]).then_inc(prep_pe, 1)
            pe.wait_ge(prep, 23)
            nc.tensor.matmul(ps_p[1][0:TN + 1, 0:1], earlier[0:TN, 0:TN + 1], plan_f[0:TN, 1:2], start=True,
                             stop=True).then_inc(prep_pe, 1)
            pe.wait_ge(prep_act, 10)
            for k in range(2):
                for n in range(4):
                    done = nc.tensor.matmul(ps_w[k][:, n * P:(n + 1) * P], wx_t[:, n, k * P:(k + 1) * P], ws_pair[:, :],
                                            start=True, stop=True)
                done.then_inc(prep_pe, 1)
            pe.wait_ge(prep, 29)
            for n in range(4):
                done = nc.tensor.matmul(ps_p[0][:, n * P:(n + 1) * P], bx_wide[:, n, :], ws_pair[:, :], start=True, stop=True)
            done.then_inc(prep_pe, 1)

            def step(it):
                u = it.back(-1)
                if u.exists():
                    s = u.slot(2)
                    pe.wait_ge(xt_kept, u.i + 1)
                    wait(pe, base_kept, u.i - 1)
                    if u.is_first():
                        pe.wait_ge(prep, 32)
                    for a in range(2):
                        for c in range(2):
                            at = (2 * a + c) * P
                            nc.tensor.matmul(ps_h[s][:, a, :], xn_t[:, s, at:at + P], w_both[:, c, :], start=(c == 0), stop=False)
                        done = nc.tensor.matmul(ps_h[s][:, a, 0:D], ident[:, :], x_tile(u.half(a)), start=False, stop=True)
                    done.then_inc(h_done, 1)
                u = it.back(-2)
                if u.exists():
                    s = u.slot(2)
                    pe.wait_ge(xn_done, u.i + 1)
                    wait(pe, xt_kept, u.i - 1)
                    if u.is_first():
                        pe.wait_ge(prep_act, 8)
                    for a in range(2):
                        for c in range(2):
                            at = (2 * a + c) * P
                            done = nc.tensor.transpose(ps_t[s][:, at:at + P], xn[:, s, a, c * P:(c + 1) * P], ident[:, :])
                    done.then_inc(xt_done, 1)
            sweep(pe, FIRST, LOOP, LOOP_END, END, 4, step, TU)

    later = ExitStack()
    sb, _, _ = keeper(later)
    wfx = sb("wfx", [P, 2, HG], f32)
    bfx = sb("bfx", [1, HG], f32)
    wqkv = sb("wqkv", [DH, 3, DH], f32)
    wo = sb("wo", [DH, H, D], f32)
    bo = sb("bo", [P, D], f32)

    with ExitStack() as two:
        sb, pb, sem = keeper(two)
        index = sb("index", [P, 2 * AHEAD], i32)
        nodes = sb("nodes", [P, 2, P], f32)
        onehot = sb("onehot", [P, 2 * AHEAD, P], bf16)
        gathered = sb("gathered", [P, 2 * RING, 3 * D + 2], bf16)
        zeros = sb("zeros", [P, D + 1], bf16)
        rdeg = sb("rdeg", [P, 2, 2], f32)
        stats = sb("stats2", [P, 6], f32)
        mv = sb("mv2", [P, 2, 2], f32)
        rough = sb("rough", [P, 7], f32)
        eps_half = sb("eps_half", [P, 1], f32)
        three_half = sb("three_half", [P, 1], f32)
        centre = sb("centre", [P, D], f32)
        part_rows = sb("part_rows", [P, P], bf16)
        b_parts = sb("b_parts", [P, HG], bf16)
        xn = sb("xn2", [P, 4, D], f32)
        xn_t = sb("xn_t2", [P, 2, 2, P], f32)
        logits = sb("logits", [P, 2, HG], f32)
        peak = sb("peak", [P, H], f32)
        weights = sb("weights", [P, 2, HG], f32)
        total = sb("total", [P, 2, H], f32)
        turned = sb("turned", [P, 2, HG], f32)
        ps_sum = [pb("ps_sum0"), pb("ps_sum1")]
        ps_x, ps_l, ps_s = pb("ps_x"), pb("ps_l"), pb("ps_s")
        ps_tok = [pb("ps_tok0"), pb("ps_tok1")]
        ps_norm = pb("ps_norm")

        consts_made = sem("consts_made2")
        landed = [sem(f"landed{j}") for j in range(2 * RING)]
        nodes_made = sem("nodes_made")
        index_ready, onehot_ready, messages_in, used = sem("index_ready"), sem("onehot_ready"), sem("messages_in"), sem("used")
        summed, add_step, mean_added, xn_ready, xt_done, xt_kept, l_done, l_step, l_ready = (
            sem("summed"), sem("add_step"), sem("mean_added"), sem("xn_ready"), sem("xt_done2"), sem("xt_kept2"),
            sem("l_done"), sem("l_step"), sem("l_ready"))
        weights_in = sem("weights_in2")
        rough_step, bias_step, centred = sem("rough_step"), sem("bias_step"), sem("centred2")
        exp_done, w_step, w_ready, tokens_done, turned_kept, sums_kept = (
            sem("exp_done"), sem("w_step"), sem("w_ready"), sem("tokens_done"), sem("turned_kept"), sem("sums_kept"))
        stored = [sem("w_stored0"), sem("w_stored1")]
        ADDS, WAYS, ROUGHS = 4, 2, 7
        LOOP, LOOP_END, END = 8, TN - 2, TN + 5
        PAIRS = (TE + 1) // 2
        PAIRS_MAX = PAIRS * TN

        def planned(eng, t, field, most):
            at = bass.ds(t.i * 4 + field, 1) if isinstance(t, Tile) else slice(t * 4 + field, t * 4 + field + 1)
            return eng.value_load(plan[0:1, at], min_val=0, max_val=most)

        def edge_columns(first, i):
            return bass.ds(nc.s_assert_within(first + i * 2, 0, TE - 1,
                                              skip_runtime_bounds_check_because="the plan names edge tiles that exist"), 2)

        block = two.enter_context(nc.Block())

        @block.sync
        def _(sp):
            sp.dma_start(wfx[:, :, :], w_fx.rearrange("(c p) n -> p c n", p=P)).then_inc(weights_in, 16)
            sp.dma_start(bfx[:, :], b_fx.rearrange("(o n) -> o n", o=1)).then_inc(weights_in, 16)
            for j, w in enumerate((w_q, w_k, w_v)):
                sp.dma_start(wqkv[:, j, :], w).then_inc(weights_in, 16)
            sp.dma_start(wo[:, :, :], w_out.rearrange("(h d) n -> d h n", d=DH)).then_inc(weights_in, 16)
            sp.dma_start(bo[:, :], b_out.rearrange("(o n) -> o n", o=1).broadcast_to([P, D])).then_inc(weights_in, 16)
            rounds = planned(sp, TN, 3, PAIRS_MAX) + 1
            with sp.Fori(0, rounds) as k:
                for j in range(AHEAD):
                    for n in range(2):
                        sp.wait_ge(landed[2 * (j % RING) + n], k * (16 * AHEAD // RING) + 16 * (j // RING + 1))
                    sp.sem_inc(messages_in, 1)
            sp.wait_ge(weights_in, 112)

        @block.gpsimd
        def _(pool):
            rounds = planned(pool, TN, 3, PAIRS_MAX) + 1
            with pool.Fori(0, rounds) as k:
                for j in range(AHEAD):
                    pool.wait_ge(index_ready, k * AHEAD + (j + 1))
                    pool.wait_ge(used, k * AHEAD + (j + 1 + AHEAD - RING))
                    pool.nop(nofuse=True)
                    for n in range(2):
                        at, slot = 2 * j + n, 2 * (j % RING) + n
                        nc.gpsimd.indirect_dma_start(
                            gathered[:, slot, 0:3 * D], None, messages,
                            bass.IndirectOffsetOnAxis(ap=index[:, at:at + 1], axis=0)).then_inc(landed[slot], 16)

        @block.scalar
        def _(act):
            nc.scalar.preload_act_table_set("natural_log_exp_and_others")
            act.wait_ge(consts_made, 4)

            def indices(t):
                first, steps, before = (planned(act, t, f, m) for f, m in ((0, TE - 1), (1, PAIRS), (2, PAIRS_MAX)))
                with act.Fori(0, steps) as i:
                    s = act.snap(before + i)
                    act.wait_ge(used, s + 1)
                    nc.scalar.copy(index[:, bass.ds(s % AHEAD * 2, 2)], src_cols[:, edge_columns(first, i)]).then_inc(index_ready, 1)

            def norm(t):
                done = t.i * ROUGHS
                act.wait_ge(add_step, t.i * ADDS + 4)
                nc.scalar.activation(rough[:, 0:1], mv[:, t.slot(2), 1:2], ACT.Identity, bias=eps_half[:, :], scale=-0.5).then_inc(rough_step, 1)
                nc.scalar.activation(rough[:, 1:2], mv[:, t.slot(2), 0:1], ACT.Copy, scale=-1.0).then_inc(rough_step, 1)
                act.wait_ge(rough_step, done + 2)
                nc.scalar.activation(rough[:, 2:3], rough[:, 0:1], ACT.Ln, scale=-2.0).then_inc(rough_step, 1)
                nc.scalar.activation(centre[:, :], x_tile(t), ACT.Identity, bias=rough[:, 1:2]).then_inc(centred, 1)
                act.wait_ge(rough_step, done + 3)
                nc.scalar.activation(rough[:, 3:4], rough[:, 2:3], ACT.Exp, scale=-0.5).then_inc(rough_step, 1)
                act.wait_ge(rough_step, done + 4)
                nc.scalar.activation(rough[:, 4:5], rough[:, 3:4], ACT.Square).then_inc(rough_step, 1)
                act.wait_ge(rough_step, done + 5)
                nc.scalar.activation(rough[:, 5:6], rough[:, 4:5], ACT.Identity, bias=three_half[:, :],
                                     scale=rough[:, 0:1]).then_inc(rough_step, 1)
                act.wait_ge(rough_step, done + 6)
                nc.scalar.activation(rough[:, 6:7], rough[:, 3:4], ACT.Identity, scale=rough[:, 5:6]).then_inc(rough_step, 1)
                wait(act, tokens_done, t.i - 3)
                act.wait_ge(centred, t.i + 1)
                act.wait_ge(rough_step, done + 7)
                nc.scalar.activation(xn[:, t.slot(4), :], centre[:, :], ACT.Identity, scale=rough[:, 6:7]).then_inc(xn_ready, 1)

            def step(it):
                if it.exists():
                    indices(it)
                if it.is_last():
                    steps = planned(act, TN, 2, PAIRS_MAX)
                    act.wait_ge(index_ready, steps)
                    act.nop(nofuse=True).then_inc(index_ready, AHEAD)
                t = it.back(3)
                if t.exists():
                    s = t.slot(2)
                    act.wait_ge(xt_done, t.i + 1)
                    wait(act, l_done, t.i - 1)
                    nc.scalar.copy(xn_t[:, s, :, :].rearrange("p a b -> p (a b)"), ps_x[:, 0:D]).then_inc(xt_kept, 1)
                t = it.back(5)
                if t.exists():
                    s = t.slot(2)
                    act.wait_ge(l_ready, t.i + 1)
                    wait(act, tokens_done, t.i - 1)
                    nc.scalar.activation(weights[:, s, :], logits[:, s, :], ACT.Exp).then_inc(exp_done, 1)
                if it.back(2).exists():
                    norm(it.back(2))
                t = it.back(6)
                if t.exists():
                    s = t.slot(2)
                    act.wait_ge(tokens_done, t.i + 1)
                    wait(act, stored[s], t.round(2) * 16)
                    nc.scalar.copy(turned[:, s, :], ps_s[:, :]).then_inc(turned_kept, 1)
                    act.wait_ge(turned_kept, t.i + 1)
                    act.dma_start(weights_t[bass.ds(t.i, 1), :, :].rearrange("o p n -> p (o n)"),
                                  turned[:, s, :]).then_inc(stored[s], 16)
            sweep(act, 0, LOOP, LOOP_END, END, 4, step)
            for s in stored:
                act.wait_ge(s, 16 * (TN // 2))

        @block.vector
        def _(dve):
            nc.vector.memset(zeros[:, :], 0.0).then_inc(consts_made, 1)
            nc.vector.memset(gathered[:, :, 3 * D:3 * D + 1], 1.0).then_inc(consts_made, 1)
            nc.vector.memset(eps_half[:, :], -0.5 * EPS).then_inc(consts_made, 1)
            nc.vector.memset(three_half[:, :], 1.5).then_inc(consts_made, 1)
            nc.vector.memset(part_rows[:, :], 0.0).then_inc(bias_step, 1)
            nc.vector.memset(b_parts[:, :], 0.0).then_inc(bias_step, 1)
            dve.wait_ge(bias_step, 2)
            done = 2
            for n in range(3):
                row = slice(32 * n, 32 * n + 1)
                nc.vector.memset(part_rows[row, :], 1.0).then_inc(bias_step, 1)
                nc.vector.tensor_copy(b_parts[row, :], b_logit[row, :]).then_inc(bias_step, 1)
                done += 2
                dve.wait_ge(bias_step, done)
                for m in range(n):
                    rest = b_logit[row, :] if m == 0 else logits[row, m - 1, :]
                    nc.vector.tensor_tensor(logits[row, m, :], rest, b_parts[row, :], ALU.subtract).then_inc(bias_step, 1)
                    dve.wait_ge(bias_step, done + 1)
                    nc.vector.tensor_copy(b_parts[row, :], logits[row, m, :]).then_inc(bias_step, 1)
                    done += 2
                    dve.wait_ge(bias_step, done)

            def onehots(t):
                first, steps, before = (planned(dve, t, f, m) for f, m in ((0, TE - 1), (1, PAIRS), (2, PAIRS_MAX)))
                shape = [P, 2, P]
                nc.vector.tensor_scalar(nodes[:, t.slot(2), :], node_row[:, :], window[:, bass.ds(t.i, 1)], None,
                                        ALU.add).then_inc(nodes_made, 1)
                dve.wait_ge(nodes_made, t.i + 1)
                dve.nop(nofuse=True)
                with dve.Fori(0, steps) as i:
                    s = dve.snap(before + i)
                    dve.wait_ge(used, s + 1)
                    nc.vector.tensor_tensor(
                        onehot[:, bass.ds(s % AHEAD * 2, 2), :], nodes[:, t.slot(2):t.slot(2) + 1, :].broadcast_to(shape),
                        dst_cols[:, edge_columns(first, i)].rearrange("p (e o) -> p e o", o=1).broadcast_to(shape),
                        ALU.is_equal).then_inc(onehot_ready, 1)

            def add_mean(t):
                s, done = t.slot(2), t.i * ADDS
                dve.wait_ge(summed, t.i + 1)
                nc.vector.tensor_scalar(rdeg[:, s, 0:1], ps_sum[s][:, D:D + 1], 1.0, None, ALU.max).then_inc(add_step, 1)
                dve.wait_ge(add_step, done + 1)
                nc.vector.reciprocal(rdeg[:, s, 1:2], rdeg[:, s, 0:1]).then_inc(add_step, 1)
                dve.wait_ge(add_step, done + 2)
                nc.vector.scalar_tensor_tensor(x_tile(t), ps_sum[s][:, 0:D], rdeg[:, s, 1:2], x_tile(t), ALU.mult,
                                               ALU.add).then_inc(mean_added, 1)
                dve.wait_ge(mean_added, t.i + 1)
                dve.nop(nofuse=True)
                nc.vector.bn_stats(stats[:, :], x_tile(t)).then_inc(add_step, 1)
                dve.wait_ge(add_step, done + 3)
                wait(dve, xn_ready, t.i - 1)
                dve.nop(nofuse=True)
                nc.vector.bn_aggr(mv[:, s, :], stats[:, :]).then_inc(add_step, 1)

            def by_head(a):
                return a.rearrange("p (h g) -> p h g", h=H)

            def wide(a):
                return a.rearrange("p (h o) -> p h o", o=1).broadcast_to([a.shape[0], H, G])

            def less_peak(t):
                s = t.slot(2)
                dve.wait_ge(l_done, t.i + 1)
                wait(dve, exp_done, t.i - 1)
                nc.vector.tensor_reduce(peak[:, :], by_head(ps_l[:, :]), AX.X, ALU.max).then_inc(l_step, 1)
                dve.wait_ge(l_step, t.i + 1)
                nc.vector.tensor_tensor(by_head(logits[:, s, :]), by_head(ps_l[:, :]), wide(peak[:, :]),
                                        ALU.subtract).then_inc(l_ready, 1)

            def normalise(t):
                s, done = t.slot(2), t.i * WAYS
                dve.wait_ge(exp_done, t.i + 1)
                nc.vector.tensor_reduce(total[:, 0, :], by_head(weights[:, s, :]), AX.X, ALU.add).then_inc(w_step, 1)
                dve.wait_ge(w_step, done + 1)
                nc.vector.reciprocal(total[:, 1, :], total[:, 0, :]).then_inc(w_step, 1)
                dve.wait_ge(w_step, done + 2)
                nc.vector.tensor_tensor(by_head(weights[:, s, :]), by_head(weights[:, s, :]), wide(total[:, 1, :]),
                                        ALU.mult).then_inc(w_ready, 1)

            def step(it):
                for back, stage in ((0, onehots), (1, add_mean), (5, normalise), (4, less_peak)):
                    if it.back(back).exists():
                        stage(it.back(back))
            sweep(dve, 0, LOOP, LOOP_END, END, 4, step)
            dve.wait_ge(tokens_done, TN)
            for c in range(2):
                nc.vector.tensor_copy(token_sum[:, c, :], ps_tok[c][:, :]).then_inc(sums_kept, 1)
            nc.vector.tensor_copy(norm_sum[:, :], ps_norm[:, :]).then_inc(sums_kept, 1)

        @block.tensor
        def _(pe):
            pe.wait_ge(consts_made, 4)
            pe.wait_ge(bias_step, 14)
            pe.nop(nofuse=True).then_inc(used, AHEAD)

            def sum_messages(t):
                steps, before = planned(pe, t, 1, PAIRS), planned(pe, t, 2, PAIRS_MAX)
                acc = ps_sum[t.slot(2)]
                wait(pe, mean_added, t.i - 1)
                nc.tensor.matmul(acc[:, 0:D + 1], zeros[:, 0:P], zeros[:, :], start=True, stop=False, skip_group_check=True)
                with pe.Fori(0, steps) as i:
                    s = pe.snap(before + i)
                    pe.wait_ge(onehot_ready, s + 1)
                    pe.wait_ge(messages_in, s + 1)
                    first = pe.snap(s % AHEAD * 2)
                    slot = pe.snap(s % RING * 2)
                    for n in range(2):
                        hot = onehot[:, bass.ds(first + n, 1), :].rearrange("p o n -> p (o n)")
                        for part in range(3):
                            width = D + (part == 2)
                            done = nc.tensor.matmul(
                                acc[:, 0:width], hot,
                                gathered[:, bass.ds(slot + n, 1), part * D:part * D + width].rearrange("p o n -> p (o n)"),
                                start=False, stop=False, skip_group_check=True)
                    done.then_inc(used, 1)
                nc.tensor.matmul(acc[:, 0:D + 1], zeros[:, 0:P], zeros[:, :], start=False, stop=True,
                                 skip_group_check=True).then_inc(summed, 1)

            def turn_x(t):
                pe.wait_ge(xn_ready, t.i + 1)
                wait(pe, xt_kept, t.i)
                for c in range(2):
                    done = nc.tensor.transpose(ps_x[:, c * P:(c + 1) * P], xn[:, t.slot(4), c * P:(c + 1) * P], ident[:, :])
                done.then_inc(xt_done, 1)

            def slice_logits(t):
                s = t.slot(2)
                pe.wait_ge(xt_kept, t.i + 1)
                wait(pe, l_ready, t.i)
                nc.tensor.matmul(ps_l[:, :], xn_t[:, s, 0, :], w_logit[:, 0, :], start=True, stop=False)
                nc.tensor.matmul(ps_l[:, :], xn_t[:, s, 1, :], w_logit[:, 1, :], start=False, stop=False)
                nc.tensor.matmul(ps_l[:, :], part_rows[:, :], b_parts[:, :], start=False, stop=True).then_inc(l_done, 1)

            def tokens(t):
                s, x4 = t.slot(2), t.slot(4)
                rows = LAST if t.is_last() else P
                pe.wait_ge(w_ready, t.i + 1)
                wait(pe, turned_kept, t.i)
                for c in range(2):
                    nc.tensor.matmul(ps_tok[c][:, :], xn[0:rows, x4, c * P:(c + 1) * P], weights[0:rows, s, :],
                                     start=t.is_first(), stop=t.is_last(), skip_group_check=True)
                nc.tensor.matmul(ps_norm[:, :], ones[0:rows, :], weights[0:rows, s, :], start=t.is_first(),
                                 stop=t.is_last(), skip_group_check=True)
                for c in range(4):
                    done = nc.tensor.transpose(ps_s[:, c * P:(c + 1) * P], weights[:, s, c * P:(c + 1) * P], ident[:, :])
                done.then_inc(tokens_done, 1)

            def step(it):
                if isinstance(it.k, int) and it.at == TN:
                    pairs, rounds_before = planned(pe, TN, 2, PAIRS_MAX), planned(pe, TN, 3, PAIRS_MAX)
                    pe.wait_ge(used, pairs + AHEAD)
                    pe.wait_ge(messages_in, rounds_before * AHEAD + (AHEAD - RING))
                    pe.nop(nofuse=True).then_inc(used, RING)
                for back, stage in ((0, sum_messages), (2, turn_x), (3, slice_logits), (5, tokens)):
                    if it.back(back).exists():
                        stage(it.back(back))
            sweep(pe, 0, LOOP, LOOP_END, END, 4, step)

    with ExitStack() as three:
        sb, pb, sem = keeper(three)
        rnorm = sb("rnorm", [DH, HG], f32)
        token = sb("token", [DH, HG], f32)
        q_t, k_t, v = sb("q_t", [DH, HG], f32), sb("k_t", [DH, HG], f32), sb("v", [G, HG], f32)
        att, att_t, o_t = sb("att", [G, HG], f32), sb("att_t", [G, HG], f32), sb("o_t", [DH, HG], f32)
        peak3, total3 = sb("peak3", [G, H], f32), sb("total3", [G, 2, H], f32)
        w_final = sb("w_final", [P, 4, D], f32)
        turned = sb("turned3", [P, 4, HG], f32)
        result = sb("result", [P, 4, D], f32)
        ps = [pb(f"ps3_{n}") for n in range(8)]
        dve_step, pe_step, act_step = sem("dve_step"), sem("pe_step"), sem("act_step")
        biased, product, added = sem("biased"), sem("product"), sem("added")
        turned_in = [sem(f"turned_in{j}") for j in range(4)]
        out_done = [sem(f"out_done{j}") for j in range(4)]
        LOOPS = TN // 4 * 4
        block = three.enter_context(nc.Block())

        @block.sync
        def _(sp):
            def load(t):
                s = t.slot(4)
                wait(sp, product, t.i - 3)
                sp.dma_start(turned[:, s, :],
                             weights_t[bass.ds(t.i, 1), :, :].rearrange("o p n -> p (o n)")).then_inc(turned_in[s], 16)
            sweep(sp, 0, 4, LOOPS, TN - 1, 4, load)

        @block.gpsimd
        def _(pool):
            def bias(t):
                nc.gpsimd.tensor_tensor(x_tile(t), x_tile(t), bo[:, :], ALU.add).then_inc(biased, 1)
            sweep(pool, 0, 0, LOOPS, TN - 1, 4, bias)

        @block.scalar
        def _(act):
            nc.scalar.preload_act_table(ACT.Exp)
            act.wait_ge(pe_step, 2)
            nc.scalar.copy(k_t[:, :], ps[2][0:DH, :]).then_inc(act_step, 1)
            act.wait_ge(dve_step, 7)
            nc.scalar.activation(att[:, :], att[:, :], ACT.Exp, scale=float(DH) ** -0.5).then_inc(act_step, 1)

            def store(t):
                s = t.slot(4)
                act.wait_ge(added, t.i + 1)
                if t.is_last():
                    act.dma_start(out[(TN - 1) * P:N, :], result[0:LAST, s, :]).then_inc(out_done[s], 16)
                else:
                    act.dma_start(out[bass.ds(t.i * P, P), :], result[:, s, :]).then_inc(out_done[s], 16)
            sweep(act, 0, 0, LOOPS, TN - 1, 4, store)
            for s in range(4):
                act.wait_ge(out_done[s], 16 * ((TN - s + 3) // 4))

        @block.vector
        def _(dve):
            def by_head(a):
                return a[:, :].rearrange("p (h g) -> p h g", h=H)

            def wide(a):
                return a.rearrange("p (h o) -> p h o", o=1).broadcast_to([a.shape[0], H, G])
            nc.vector.tensor_scalar(rnorm[:, :], norm_sum[0:DH, :], 1e-5, None, ALU.add).then_inc(dve_step, 1)
            dve.wait_ge(dve_step, 1)
            nc.vector.reciprocal(rnorm[:, :], rnorm[:, :]).then_inc(dve_step, 1)
            dve.wait_ge(dve_step, 2)
            dve.wait_ge(pe_step, 1)
            nc.vector.tensor_tensor(token[:, :], ps[0][0:DH, :], rnorm[:, :], ALU.mult).then_inc(dve_step, 1)
            dve.wait_ge(pe_step, 2)
            nc.vector.tensor_copy(q_t[:, :], ps[1][0:DH, :]).then_inc(dve_step, 1)
            dve.wait_ge(pe_step, 3)
            nc.vector.tensor_copy(v[:, :], ps[3][0:G, :]).then_inc(dve_step, 1)
            dve.wait_ge(pe_step, 4)
            nc.vector.tensor_reduce(peak3[:, :], ps[4][0:G, :].rearrange("p (h g) -> p h g", h=H), AX.X, ALU.max).then_inc(dve_step, 1)
            dve.wait_ge(dve_step, 6)
            nc.vector.tensor_tensor(by_head(att), ps[4][0:G, :].rearrange("p (h g) -> p h g", h=H), wide(peak3[:, :]),
                                    ALU.subtract).then_inc(dve_step, 1)
            dve.wait_ge(act_step, 2)
            nc.vector.tensor_reduce(total3[:, 0, :], by_head(att), AX.X, ALU.add).then_inc(dve_step, 1)
            dve.wait_ge(dve_step, 8)
            nc.vector.reciprocal(total3[:, 1, :], total3[:, 0, :]).then_inc(dve_step, 1)
            dve.wait_ge(dve_step, 9)
            nc.vector.tensor_tensor(by_head(att), by_head(att), wide(total3[:, 1, :]), ALU.mult).then_inc(dve_step, 1)
            dve.wait_ge(pe_step, 5)
            nc.vector.tensor_copy(att_t[:, :], ps[5][0:G, :]).then_inc(dve_step, 1)
            dve.wait_ge(pe_step, 6)
            nc.vector.tensor_copy(o_t[:, :], ps[0][0:DH, :]).then_inc(dve_step, 1)
            dve.wait_ge(pe_step, 7)
            for n in range(2):
                nc.vector.tensor_copy(w_final[:, 2 * n:2 * n + 2, :],
                                      ps[6 + n][:, :].rearrange("p (c d) -> p c d", c=2)).then_inc(dve_step, 1)

            def add(t):
                s = t.slot(4)
                dve.wait_ge(biased, t.i + 1)
                wait(dve, out_done[s], t.round(4) * 16)
                dve.wait_ge(product, t.i + 1)
                nc.vector.tensor_tensor(result[:, s, :], ps[s][:, 0:D], x_tile(t), ALU.add).then_inc(added, 1)
            sweep(dve, 0, 4, LOOPS, TN - 1, 4, add)

        @block.tensor
        def _(pe):
            def head(h):
                return slice(h * G, (h + 1) * G)
            for h in range(H):
                for c in range(2):
                    nc.tensor.matmul(ps[0][0:DH, head(h)], wfx[:, c, head(h)], token_sum[:, c, head(h)], start=(c == 0), stop=False)
                done = nc.tensor.matmul(ps[0][0:DH, head(h)], bfx[0:1, head(h)], norm_sum[0:1, head(h)], start=False, stop=True)
            done.then_inc(pe_step, 1)
            pe.wait_ge(dve_step, 3)
            nc.tensor.matmul(ps[1][0:DH, :], wqkv[:, 0, :], token[:, :], start=True, stop=True)
            nc.tensor.matmul(ps[2][0:DH, :], wqkv[:, 1, :], token[:, :], start=True, stop=True).then_inc(pe_step, 1)
            for h in range(H):
                done = nc.tensor.matmul(ps[3][0:G, head(h)], token[:, head(h)], wqkv[:, 2, :], start=True, stop=True)
            done.then_inc(pe_step, 1)
            pe.wait_ge(dve_step, 4)
            pe.wait_ge(act_step, 1)
            for h in range(H):
                done = nc.tensor.matmul(ps[4][0:G, head(h)], q_t[:, head(h)], k_t[:, head(h)], start=True, stop=True)
            done.then_inc(pe_step, 1)
            pe.wait_ge(dve_step, 10)
            for h in range(H):
                done = nc.tensor.transpose(ps[5][0:G, head(h)], att[:, head(h)], ident[0:G, 0:G])
            done.then_inc(pe_step, 1)
            pe.wait_ge(dve_step, 11)
            for h in range(H):
                done = nc.tensor.matmul(ps[0][0:DH, head(h)], v[:, head(h)], att_t[:, head(h)], start=True, stop=True)
            done.then_inc(pe_step, 1)
            pe.wait_ge(dve_step, 12)
            for h in range(H):
                c, r = h // 2, h % 2 * G
                done = nc.tensor.matmul(ps[6 + c // 2][r:r + G, c % 2 * D:(c % 2 + 1) * D], o_t[:, head(h)], wo[:, h, :],
                                        start=True, stop=True)
            done.then_inc(pe_step, 1)
            pe.wait_ge(dve_step, 14)

            def multiply(t):
                s = t.slot(4)
                pe.wait_ge(turned_in[s], t.round(4) * 16 + 16)
                wait(pe, added, t.i - 3)
                for c in range(4):
                    done = nc.tensor.matmul(ps[s][:, 0:D], turned[:, s, c * P:(c + 1) * P], w_final[:, c, :],
                                            start=(c == 0), stop=(c == 3))
                done.then_inc(product, 1)
            sweep(pe, 0, 4, LOOPS, TN - 1, 4, multiply)

    later.close()
    whole.close()


INPUTS = ['x', 'src', 'dst', 'L0_gnn_W_self', 'L0_gnn_W_neigh', 'L0_ffn_W_fx', 'L0_ffn_b_fx', 'L0_ffn_W_x',
          'L0_ffn_b_x', 'L0_ffn_W_slice', 'L0_ffn_b_slice', 'L0_ffn_W_q', 'L0_ffn_W_k', 'L0_ffn_W_v',
          'L0_ffn_W_out', 'L0_ffn_b_out', 'L0_ffn_temperature']


def kernel(**inputs):
    import concourse.bacc as bacc
    from concourse.bass_utils import run_bass_kernel_spmd

    nc = bacc.Bacc("TRN2", target_bir_lowering=False, num_devices=1)
    arrays, args = {}, []
    for name in INPUTS:
        a = np.ascontiguousarray(inputs[name])
        arrays[f"in_{name}"] = a
        args.append(nc.dram_tensor(f"in_{name}", a.shape, mybir.dt.from_np(a.dtype), kind="ExternalInput").ap())
    out = nc.dram_tensor("out", (N, D), mybir.dt.float32, kind="ExternalOutput").ap()
    build(nc, *args, out)
    return run_bass_kernel_spmd(nc, [arrays], core_ids=[0]).results[0]["out"]
```
